# Optimizing a Trainium2 kernel written in Bass

```python
import numpy as np
import jax
import jax.numpy as jnp

def _softmax(x, axis=-1):
    return jax.nn.softmax(x, axis=axis)

def _gelu(x):
    return jax.nn.gelu(x, approximate=True)

def _silu(x):
    return jax.nn.silu(x)

def _sigmoid(x):
    return jax.nn.sigmoid(x)

def _layernorm(x, axis=-1, eps=1e-05):
    m = jnp.mean(x, axis=axis, keepdims=True)
    v = jnp.var(x, axis=axis, keepdims=True)
    return (x - m) / jnp.sqrt(v + eps)

def _scatter_add(tgt, idx, src, axis=0):
    return tgt.at[idx].add(src)

def _segment_sum(src, seg, n):
    return jax.ops.segment_sum(src, seg, n)
kernel_name = 'mk_gnn_preln_d2_gnn_r32_464394'

def setup_inputs(seed: int=0):
    np.random.seed(seed)
    _w = jnp.asarray

    def _rec_inputs():
        import jax
        import jax.numpy as jnp
        _gk = jax.random.key(seed)
        x = -0.000202 + 1 * jax.random.normal(jax.random.fold_in(_gk, 1), (50000, 128), jnp.float32)
        src = jax.random.randint(jax.random.fold_in(_gk, 2), (50000,), 0, 50000, jnp.int32)
        dst = jnp.minimum((50000 * jax.random.uniform(jax.random.fold_in(_gk, 3), (50000,)) ** 2.0).astype(jnp.int32), 49999)
        _o = jnp.argsort(dst, stable=True)
        src = src[_o]
        dst = dst[_o]
        edge_attr_128 = 2.93046e-05 + 1.00006 * jax.random.normal(jax.random.fold_in(_gk, 13), (50000, 128), jnp.float32)
        return (x, src, dst, edge_attr_128)
    x, src, dst, edge_attr_128 = _rec_inputs()

    def _L0_gnn_setup():
        import jax, jax.numpy as jnp
        import numpy as np
        N_NODES = 50000
        N_EDGES = 25000
        D_FEAT = 128
        EPS = 1e-12
        key = jax.random.key(seed)
        k1, k2, k3 = jax.random.split(key, 3)
        feat = jax.random.normal(k1, (N_NODES, D_FEAT), dtype=jnp.float32)
        beta = jnp.ones((1,), dtype=jnp.float32)
        src = jax.random.randint(k2, (N_EDGES,), 0, N_NODES, dtype=jnp.int32)
        dst = jax.random.randint(k3, (N_EDGES,), 0, N_NODES, dtype=jnp.int32)
        return {'feat': feat, 'beta': beta, 'src': src, 'dst': dst}
    _L0_gnn_all = _L0_gnn_setup()
    _L0_gnn_in = {k: v for k, v in _L0_gnn_all.items() if k in ('beta',)}
    del _L0_gnn_all

    def _L1_gnn_setup():
        import jax, jax.numpy as jnp
        import numpy as np
        N_NODES = 50000
        N_EDGES = 20000
        C = 128
        BN_EPS = 0.0001

        def elu(x):
            return jnp.where(x > 0, x, jnp.expm1(x))

        def batchnorm_train(x, gamma, beta):
            mean = jnp.mean(x, axis=0)
            var = jnp.mean((x - mean) ** 2, axis=0)
            return gamma * (x - mean) * jax.lax.rsqrt(var + BN_EPS) + beta
        key = jax.random.key(seed)
        ks = jax.random.split(key, 8)
        x = jax.random.normal(ks[0], (N_NODES, C), dtype=jnp.float32)
        edge_index = jax.random.randint(ks[1], (2, N_EDGES), 0, N_NODES, dtype=jnp.int32)
        edge_attr = jax.random.normal(ks[2], (N_EDGES, C), dtype=jnp.float32)
        u = jax.random.normal(ks[3], (1, C), dtype=jnp.float32)
        batch = jnp.zeros((N_NODES,), dtype=jnp.int32)
        s1 = 1.0 / np.sqrt(2 * C)
        W1 = jax.random.uniform(ks[4], (2 * C, C), jnp.float32, -s1, s1)
        b1 = jnp.zeros((C,), jnp.float32)
        g1 = jnp.ones((C,), jnp.float32)
        be1 = jnp.zeros((C,), jnp.float32)
        W2 = jax.random.uniform(ks[5], (2 * C, C), jnp.float32, -s1, s1)
        b2 = jnp.zeros((C,), jnp.float32)
        g2 = jnp.ones((C,), jnp.float32)
        be2 = jnp.zeros((C,), jnp.float32)
        return dict(x=x, edge_index=edge_index, edge_attr=edge_attr, u=u, batch=batch, W1=W1, b1=b1, g1=g1, be1=be1, W2=W2, b2=b2, g2=g2, be2=be2)
    _L1_gnn_all = _L1_gnn_setup()
    _L1_gnn_in = {k: v for k, v in _L1_gnn_all.items() if k in ('u', 'W1', 'b1', 'g1', 'be1', 'W2', 'b2', 'g2', 'be2')}
    del _L1_gnn_all
    return {'x': x, 'src': src, 'dst': dst, 'edge_attr_128': edge_attr_128, 'L0_gnn_beta': _L0_gnn_in['beta'], 'L1_gnn_u': _L1_gnn_in['u'], 'L1_gnn_W1': _L1_gnn_in['W1'], 'L1_gnn_b1': _L1_gnn_in['b1'], 'L1_gnn_g1': _L1_gnn_in['g1'], 'L1_gnn_be1': _L1_gnn_in['be1'], 'L1_gnn_W2': _L1_gnn_in['W2'], 'L1_gnn_b2': _L1_gnn_in['b2'], 'L1_gnn_g2': _L1_gnn_in['g2'], 'L1_gnn_be2': _L1_gnn_in['be2']}

def reference(x, src, dst, edge_attr_128, L0_gnn_beta, L1_gnn_u, L1_gnn_W1, L1_gnn_b1, L1_gnn_g1, L1_gnn_be1, L1_gnn_W2, L1_gnn_b2, L1_gnn_g2, L1_gnn_be2):
    import jax
    import jax.numpy as jnp

    def _L0_gnn_ref(feat, beta, src, dst):
        import jax, jax.numpy as jnp
        import numpy as np
        N_NODES = 50000
        N_EDGES = 25000
        D_FEAT = 128
        EPS = 1e-12
        norm = jnp.maximum(jnp.linalg.norm(feat, axis=-1, keepdims=True), EPS)
        norm_h = feat / norm
        cos = jnp.sum(norm_h[src] * norm_h[dst], axis=-1)
        e = beta[0] * cos
        m = jax.ops.segment_max(e, dst, num_segments=N_NODES)
        m = jax.lax.stop_gradient(m)
        e_exp = jnp.exp(e - m[dst])
        denom = jax.ops.segment_sum(e_exp, dst, num_segments=N_NODES)
        p = e_exp / denom[dst]
        msgs = feat[src] * p[:, None]
        out = jax.ops.segment_sum(msgs, dst, num_segments=N_NODES)
        return out

    def _L1_gnn_ref(x, edge_index, edge_attr, u, batch, W1, b1, g1, be1, W2, b2, g2, be2):
        import jax, jax.numpy as jnp
        import numpy as np
        N_NODES = 50000
        N_EDGES = 20000
        C = 128
        BN_EPS = 0.0001

        def elu(x):
            return jnp.where(x > 0, x, jnp.expm1(x))

        def batchnorm_train(x, gamma, beta):
            mean = jnp.mean(x, axis=0)
            var = jnp.mean((x - mean) ** 2, axis=0)
            return gamma * (x - mean) * jax.lax.rsqrt(var + BN_EPS) + beta
        row, col = (edge_index[0], edge_index[1])
        h = jnp.concatenate([x[row], edge_attr], axis=1)
        h = elu(batchnorm_train(h @ W1 + b1, g1, be1))
        sums = jax.ops.segment_sum(h, col, num_segments=x.shape[0])
        cnt = jax.ops.segment_sum(jnp.ones((h.shape[0],), h.dtype), col, num_segments=x.shape[0])
        agg = sums / jnp.maximum(cnt, 1.0)[:, None]
        z = jnp.concatenate([x, agg], axis=1)
        return elu(batchnorm_train(z @ W2 + b2, g2, be2))
    edge_index = jnp.stack([src, dst])
    batch0 = jnp.zeros((50000,), jnp.int32)
    h = jnp.maximum(_layernorm(x, axis=-1), 0.0)
    x = x + _L0_gnn_ref(h, L0_gnn_beta, src, dst)
    h = jnp.maximum(_layernorm(x, axis=-1), 0.0)
    x = x + _L1_gnn_ref(h, edge_index, edge_attr_128, L1_gnn_u, batch0, L1_gnn_W1, L1_gnn_b1, L1_gnn_g1, L1_gnn_be1, L1_gnn_W2, L1_gnn_b2, L1_gnn_g2, L1_gnn_be2)
    return x

_drawn_inputs = setup_inputs


def setup_inputs(seed=0):
    import zlib

    import numpy as np

    out = dict(_drawn_inputs(seed))
    spreads = {'L1_gnn_b1': (0.0, 0.1),
     'L1_gnn_g1': (1.0, 0.2),
     'L1_gnn_be1': (0.0, 0.1),
     'L1_gnn_b2': (0.0, 0.1),
     'L1_gnn_g2': (1.0, 0.2),
     'L1_gnn_be2': (0.0, 0.1)}
    factors = {}
    for name, (base, spread) in spreads.items():
        noise = np.random.default_rng([zlib.crc32(name.encode()), seed]).standard_normal(out[name].shape)
        drawn = base * np.exp(spread * noise) if base else spread * noise
        out[name] = jnp.asarray(drawn.astype(out[name].dtype))
    for name, factor in factors.items():
        out[name] = (out[name] * factor).astype(out[name].dtype)
    return out
```

```python
from contextlib import ExitStack

import concourse.bass as bass
from concourse import mybir

P = 128
TPG = 4
RING = 4
GW = P * TPG
FAR = float(2 ** 20)
LOWEST = -3.0e38
LN_EPS = 1e-5
BN_EPS = 1e-4
NORM_EPS = 1e-12


def build_gnn(nc, x, src, dst, edge_attr, beta, W1, b1, g1, be1, W2, b2, g2, be2, out):
    fp32, i32 = mybir.dt.float32, mybir.dt.int32
    ALU, ACT = mybir.AluOpType, mybir.ActivationFunctionType
    N, D = x.shape
    E = src.shape[0]
    assert D == P and E == N
    G = -(-N // GW)
    assert G >= 2 * RING + 4
    T = G * TPG
    TAIL = N - (G - 1) * GW
    TAIL_FULL, TAIL_REST = TAIL // P, TAIL % P
    TB = -(-T // P)
    AUG = D + 1

    ctx = ExitStack()
    with ctx:
        def sb(name, shape, dt=fp32):
            return ctx.enter_context(nc.sbuf_tensor(name, shape, dt))

        def sem(name):
            return ctx.enter_context(nc.semaphore(name))

        def dram(name, shape):
            return nc.dram_tensor(name, shape, fp32, kind="Internal").ap()

        x1 = dram("x1", [N, D])
        agg = dram("agg", [N, D])
        y1 = dram("y1", [P, G * GW])
        y2 = dram("y2", [P, G * GW])

        wait_carrier = sem("wait_carrier")
        ps = [ctx.enter_context(nc.psum_tensor(f"bank{i}", [P, GW], fp32)) for i in range(8)]

        ident = sb("ident", [P, P])
        pick_last = sb("pick_last", [P, P])
        shift_up = sb("shift_up", [P, P])
        wrap_up = sb("wrap_up", [P, P])
        minus_half = sb("minus_half", [P, 3 * TPG])
        edge_f = sb("edge_f", [P, G, 3, TPG])
        edge_i = sb("edge_i", [P, G, 3, TPG], i32)
        slot_f = sb("slot_f", [P, RING, 3, TPG])
        slot_i = sb("slot_i", [P, RING, 3, TPG], i32)
        w1_sb = sb("w1_sb", [P, 2, D])
        w2_sb = sb("w2_sb", [P, 2, D])
        params = sb("params", [P, 7])
        bn_sum = sb("bn_sum", [P, G, 6])
        bn_mv = sb("bn_mv", [P, 2])
        bn_s = sb("bn_s", [P, 1])
        bn_t = sb("bn_t", [P, 1])
        bn_tmp = sb("bn_tmp", [P, 1])
        bn_rstd = sb("bn_rstd", [P, 1])

        def pipeline(*parts):
            eng, parts = parts[0], parts[1:]

            def step(g, u):
                for part, ahead in parts:
                    j = g + ahead
                    if not isinstance(j, int) or 0 <= j < G:
                        part(j, (u + ahead) % RING)
            first, most, least = RING, max(a for _, a in parts), min(a for _, a in parts)
            stop = first + (G - 1 - most - first) // RING * RING
            for g in range(-most, first):
                step(g, g % RING)
            with eng.Fori(first // RING, stop // RING) as turn:
                for u in range(RING):
                    step(turn * RING + u, u)
            for g in range(stop, G - least):
                step(g, g % RING)

        def wait(eng, s, value):
            if not isinstance(value, int) or value > 0:
                eng.wait_ge(s, value)

        def wait_apart(eng, *waits):
            for s, v in waits:
                wait(eng, s, v)
            if any(not isinstance(v, int) for _, v in waits):
                eng.sem_inc(wait_carrier, 1)

        def is_tail(g):
            return isinstance(g, int) and g == G - 1

        def laps(g, u, per):
            return (g - u) * (per // RING) + per

        def load_slots(j, u, ready, sem_scattered=None):
            if sem_scattered is not None:
                wait(nc.vector, sem_scattered[u], laps(j, u, 16 * TPG) - 16 * TPG)
            nc.vector.tensor_copy(slot_f[:, u, :, :], edge_f[:, bass.ds(j, 1), :, :].rearrange("p o a k -> p (o a) k"))
            nc.vector.tensor_copy(slot_i[:, u, :, :],
                                  edge_i[:, bass.ds(j, 1), :, :].rearrange("p o a k -> p (o a) k")).then_inc(ready, 1)

        def row_moves(dram_rows, tile, g, load):
            if is_tail(g):
                r0 = g * GW
                full = dram_rows[r0:r0 + TAIL_FULL * P, :].rearrange("(k p) f -> p k f", p=P)
                rest = dram_rows[r0 + TAIL_FULL * P:N, :]
                pieces = [(full, tile[:, 0:TAIL_FULL, :]), (rest, tile[0:TAIL_REST, TAIL_FULL, :])]
            else:
                pieces = [(dram_rows[bass.ds(g * GW, GW), :].rearrange("(k p) f -> p k f", p=P), tile)]
            return [(b, a) if load else (a, b) for a, b in pieces]

        with ExitStack() as c1:
            def sb1(name, shape, dt=fp32):
                return c1.enter_context(nc.sbuf_tensor(name, shape, dt))

            def sem1(name):
                return c1.enter_context(nc.semaphore(name))
            raw_i = sb1("raw_i", [P, 2, TB, P], i32)
            raw_f = sb1("raw_f", [P, 2, TB, P])
            dst_f = sb1("dst_f", [P, TB * P])
            same = sb1("same", [P, TB * P])
            last = sb1("last", [P, TB * P])
            far = sb1("far", [P, TB * P])
            zeros = sb1("zeros", [P, 4096])
            raw_set, raw_in = sem1("raw_set"), sem1("raw_in")
            const_set, const_ready = sem1("const_set"), sem1("const_ready")
            small_in = sem1("small_in")
            as_float, turned, placed = sem1("as_float"), sem1("turned"), sem1("placed")
            neigh, table_step = sem1("neigh"), sem1("table_step")
            x1_init, agg_zero, zeros_set = sem1("x1_init"), sem1("agg_zero"), sem1("zeros_set")

            with nc.Block() as block:
                @block.sync
                def _(sp):
                    step = -(-N // 8)
                    for a in range(0, N, step):
                        b = min(N, a + step)
                        sp.dma_start(x1[a:b, :], x[a:b, :]).then_inc(x1_init, 16)
                    sp.wait_ge(raw_set, 2)
                    for j, idx in ((0, src), (1, dst)):
                        for b in range(TB):
                            r0, r1 = b * P, min((b + 1) * P, E // P)
                            if r1 > r0:
                                sp.dma_start(raw_i[0:r1 - r0, j, b, :],
                                             idx[r0 * P:r1 * P].rearrange("(r c) -> r c", c=P)).then_inc(raw_in, 16)
                        r = E // P
                        sp.dma_start(raw_i[r % P:r % P + 1, j, r // P, 0:E % P],
                                     idx[r * P:E].rearrange("(r c) -> r c", r=1)).then_inc(raw_in, 16)
                    for j, v in enumerate((b1, g1, be1, b2, g2, be2)):
                        sp.dma_start(params[:, j:j + 1], v.rearrange("(p o) -> p o", o=1)).then_inc(small_in, 16)
                    sp.dma_start(params[:, 6:7], beta.rearrange("(p o) -> p o", p=1).broadcast_to([P, 1])).then_inc(small_in, 16)
                    sp.dma_start(w1_sb[:, :, :], W1.rearrange("(h k) c -> k h c", h=2)).then_inc(small_in, 16)
                    sp.dma_start(w2_sb[:, :, :], W2.rearrange("(h k) c -> k h c", h=2)).then_inc(small_in, 16)
                    sp.wait_ge(zeros_set, 1)
                    rows = 32 * P
                    n_full = N // rows
                    for z in range(n_full):
                        sp.dma_start(agg[z * rows:(z + 1) * rows, :].rearrange("(p r) f -> p (r f)", p=P),
                                     zeros[:, :]).then_inc(agg_zero, 16)
                    left = N - n_full * rows
                    zq = 16
                    while left % zq:
                        zq -= 1
                    for a in range(n_full * rows, N, 16 * 32):
                        b = min(N, a + 16 * 32)
                        q = 16 if (b - a) % 16 == 0 else 1
                        sp.dma_start(agg[a:b, :].rearrange("(p r) f -> p (r f)", p=q),
                                     zeros[0:q, 0:(b - a) // q * D]).then_inc(agg_zero, 16)
                        n_full += 1
                    sp.wait_ge(small_in, 9 * 16)
                    sp.wait_ge(x1_init, 8 * 16)
                    sp.wait_ge(agg_zero, n_full * 16)

                @block.gpsimd
                def _(pool):
                    nc.gpsimd.memset(raw_i[:, 0, :, :], 0).then_inc(raw_set, 1)
                    nc.gpsimd.memset(raw_i[:, 1, :, :], int(FAR)).then_inc(raw_set, 1)
                    nc.gpsimd.memset(minus_half[:, :], -0.5)
                    for m in (ident, pick_last, shift_up, wrap_up):
                        nc.gpsimd.memset(m[:, :], 0.0).then_inc(const_set, 1)
                    pool.wait_ge(const_set, 4)
                    for m, base in ((ident, 0), (shift_up, -1)):
                        nc.gpsimd.affine_select(out=m[:, :], in_=m[:, :], compare_op=ALU.not_equal, fill=1.0,
                                                base=base, pattern=[[-1, P]],
                                                channel_multiplier=1).then_inc(const_ready, 1)
                    nc.gpsimd.affine_select(out=pick_last[:, :], in_=pick_last[:, :], compare_op=ALU.not_equal,
                                            fill=1.0, base=-(P - 1), pattern=[[0, P]],
                                            channel_multiplier=1).then_inc(const_ready, 1)
                    nc.gpsimd.affine_select(out=wrap_up[:, P - 1:P], in_=wrap_up[:, P - 1:P],
                                            compare_op=ALU.not_equal, fill=1.0, base=0, pattern=[[0, 1]],
                                            channel_multiplier=1).then_inc(const_ready, 1)

                @block.vector
                def _(dve):
                    nc.vector.memset(zeros[:, :], 0.0).then_inc(zeros_set, 1)
                    dve.wait_ge(raw_in, 16 * 2 * (-(-(E // P) // P) + 1))
                    nc.vector.tensor_copy(raw_f[:, :, :, :], raw_i[:, :, :, :]).then_inc(as_float, 1)
                    dve.wait_ge(turned, 1)
                    nc.vector.tensor_copy(edge_i[:, :, 0, :],
                                          ps[0][:, 0:T].rearrange("p (g k) -> p g k", k=TPG)).then_inc(placed, 1)
                    nc.vector.tensor_copy(dst_f[:, :], ps[1][:, 0:TB * P]).then_inc(placed, 1)
                    dve.wait_ge(placed, 2)
                    dst_g = dst_f[:, 0:T].rearrange("p (g k) -> p g k", k=TPG)
                    nc.vector.tensor_copy(edge_f[:, :, 0, :], dst_g)
                    nc.vector.tensor_scalar(edge_i[:, :, 1, :], dst_g, float(N - 1), None, ALU.min)
                    dve.wait_ge(neigh, 1)
                    nc.vector.memset(same[:, 0:1], 0.0)
                    nc.vector.tensor_tensor(same[:, 1:T], dst_f[:, 1:T], ps[2][:, 0:T - 1],
                                            ALU.is_equal).then_inc(table_step, 1)
                    nc.vector.tensor_tensor(last[:, 0:T], dst_f[:, 0:T], ps[3][:, 0:T],
                                            ALU.is_equal).then_inc(table_step, 1)
                    dve.wait_ge(table_step, 2)
                    same_g = same[:, 0:T].rearrange("p (g k) -> p g k", k=TPG)
                    nc.vector.tensor_copy(edge_f[:, :, 2, :], same_g)
                    nc.vector.tensor_scalar(edge_f[:, :, 1, :], same_g, 1.0, -LOWEST, ALU.subtract, ALU.mult)
                    nc.vector.scalar_tensor_tensor(far[:, 0:T], last[:, 0:T], FAR, dst_f[:, 0:T],
                                                   ALU.mult, ALU.add).then_inc(table_step, 1)
                    dve.wait_ge(table_step, 3)
                    nc.vector.tensor_copy(edge_i[:, :, 2, :],
                                          far[:, 0:T].rearrange("p (g k) -> p g k", k=TPG))

                @block.tensor
                def _(pe):
                    pe.wait_ge(const_ready, 4)
                    pe.wait_ge(as_float, 1)
                    for j in range(2):
                        for b in range(TB):
                            t = nc.tensor.transpose(ps[j][:, b * P:(b + 1) * P], raw_f[:, j, b, :], ident[:, :])
                    t.then_inc(turned, 1)
                    pe.wait_ge(placed, 2)
                    nc.tensor.matmul(ps[2][:, 0:T], pick_last[:, :], dst_f[:, 0:T], start=True, stop=True)
                    nc.tensor.matmul(ps[3][:, 0:T], shift_up[:, :], dst_f[:, 0:T], start=True, stop=False)
                    nc.tensor.matmul(ps[3][:, 0:T], wrap_up[:, :], dst_f[:, 1:T + 1], start=False,
                                     stop=True).then_inc(neigh, 1)

        with ExitStack() as c1:
            def sb1(name, shape, dt=fp32):
                return c1.enter_context(nc.sbuf_tensor("p1_" + name, shape, dt))

            def sem1(name):
                return c1.enter_context(nc.semaphore("p1_" + name))
            xs = sb1("xs", [P, RING, TPG, D])
            xd = sb1("xd", [P, RING, TPG, D])
            hs = sb1("hs", [P, 2, TPG, AUG])
            hd = sb1("hd", [P, 2, TPG, D])
            junk_a = sb1("junk_a", [P, D])
            junk_v = sb1("junk_v", [P, D])
            st6 = sb1("st6", [P, 2, TPG, 6])
            mv = sb1("mv", [P, 2, TPG, 2])
            neg_mean = sb1("neg_mean", [P, 2, 2, TPG])
            var_eps = sb1("var_eps", [P, 2, TPG])
            sq = sb1("sq", [P, 2, 2, TPG])
            dot = sb1("dot", [P, 2, TPG])
            rs_in = sb1("rs_in", [P, 2, 3, TPG])
            rs = sb1("rs", [P, 2, 3, TPG])
            half = sb1("half", [P, TPG])
            score = sb1("score", [P, 2, TPG])
            pen = sb1("pen", [P, TPG, D])
            smax = sb1("smax", [P, TPG])
            ev = sb1("ev", [P, TPG, 2])
            pw = sb1("pw", [P, 2, TPG, 2])
            p_rstd = sb1("p_rstd", [P, TPG])
            wsel = sb1("wsel", [P, TPG, D])
            part = sb1("part", [P, 2, AUG])
            acc = sb1("acc", [P, 2, AUG])
            rden = sb1("rden", [P, TPG])
            rows = sb1("rows", [P, 2, TPG, D])
            D_ps, E_ps, U_ps = [ps[0], ps[1]], [ps[2], ps[3]], [ps[4], ps[5]]
            C_ps, M_ps = ps[6], ps[7]

            carry_set, idx_ready = sem1("carry_set"), sem1("idx_ready")
            gathered = [sem1(f"gathered{u}") for u in range(RING)]
            scattered = [sem1(f"scattered{u}") for u in range(RING)]
            st_done, mv_done, mean_done, v_eps_done = (sem1(n) for n in ("st_done", "mv_done", "mean_done", "v_eps_done"))
            h_done, sq_done, dot_done = sem1("h_done"), sem1("sq_done"), sem1("dot_done")
            rs_in_done, rs_done, half_done, score_done = (sem1(n) for n in ("rs_in_done", "rs_done", "half_done", "score_done"))
            aug_done = sem1("aug_done")
            drow_done, erow_done, pen_done = sem1("drow_done"), sem1("erow_done"), sem1("pen_done")
            ev_set, cm_done, v_done, max_done, ev_done = (sem1(n) for n in ("ev_set", "cm_done", "v_done", "max_done", "ev_done"))
            pw_done, p_rstd_done, wsel_done = sem1("pw_done"), sem1("p_rstd_done"), sem1("wsel_done")
            u_done, part_done, cu_done, acc_done = sem1("u_done"), sem1("part_done"), sem1("cu_done"), sem1("acc_done")
            rden_done, row_done = sem1("rden_done"), sem1("row_done")

            with nc.Block() as block:
                @block.gpsimd
                def _(pool):
                    last_row = pool.to_reg(N - 1)

                    def gather(g, u):
                        wait_apart(pool, (idx_ready, g + 1), (row_done, (g - RING + 1) * TPG))
                        for k in range(TPG):
                            for rows_to, col in ((xs, 0), (xd, 1)):
                                nc.gpsimd.indirect_dma_start(
                                    rows_to[:, u, k, :], None, x,
                                    bass.IndirectOffsetOnAxis(ap=slot_i[:, u, col, k:k + 1], axis=0),
                                    bounds_check=last_row, oob_is_err=False).then_inc(gathered[u], 16)

                    def rsqrt(g, u):
                        wait(pool, rs_in_done, g + 1)
                        wait(pool, wsel_done, (g - 1) * TPG)
                        nc.gpsimd.tensor_tensor(rs[:, u % 2, :, :], rs_in[:, u % 2, :, :],
                                                minus_half[:, :].rearrange("p (a k) -> p a k", k=TPG),
                                                ALU.pow).then_inc(rs_done, 1)

                    def scatter(g, u):
                        for k in range(TPG):
                            wait_apart(pool, (row_done, g * TPG + k + 1))
                            nc.gpsimd.indirect_dma_start(
                                x1, bass.IndirectOffsetOnAxis(ap=slot_i[:, u, 2, k:k + 1], axis=0),
                                rows[:, u % 2, k, :], None, bounds_check=last_row,
                                oob_is_err=False).then_inc(scattered[u], 16)
                    pipeline(pool, (gather, 2), (rsqrt, 0), (scatter, -1))
                    for u in range(RING):
                        pool.wait_ge(scattered[u], 16 * TPG * len(range(u, G, RING)))

                @block.scalar
                def _(act):
                    def center(g, u):
                        s = u % 2
                        wait(act, mean_done, g + 1)
                        wait(act, u_done, (g - 1) * TPG)
                        wait(act, dot_done, (g - 1) * TPG)
                        wait(act, rs_in_done, g - 1)
                        for k in range(TPG):
                            for j, (a, h) in enumerate(((xs, hs), (xd, hd))):
                                nc.scalar.activation(h[:, s, k, 0:D], a[:, u, k, :], ACT.Relu,
                                                     bias=neg_mean[:, s, j, k:k + 1]).then_inc(h_done, 1)
                        for k in range(TPG):
                            for j, h in enumerate((hs, hd)):
                                wait(act, h_done, g * 2 * TPG + 2 * k + j + 1)
                                wait(act, sq_done, g * 2 * TPG + 2 * k + j)
                                nc.scalar.activation(junk_a[:, :], h[:, s, k, 0:D], ACT.Square,
                                                     accum_out=sq[:, s, j, k:k + 1]).then_inc(sq_done, 1)

                    def weigh(g, u):
                        s = u % 2
                        wait(act, acc_done, (g - 1) * TPG)
                        for k in range(TPG):
                            wait(act, ev_done, g * TPG + k + 1)
                            nc.scalar.activation(pw[:, s, k, :], ev[:, k, :], ACT.Exp).then_inc(pw_done, 1)
                        for k in range(TPG):
                            wait(act, u_done, g * TPG + k + 1)
                            wait(act, acc_done, g * TPG + k - 1)
                            nc.scalar.copy(part[:, k % 2, :], U_ps[k % 2][:, 0:AUG]).then_inc(part_done, 1)
                    pipeline(act, (center, 1), (weigh, 0))

                @block.vector
                def _(dve):
                    nc.vector.memset(acc[:, (TPG - 1) % 2, :], 0.0).then_inc(carry_set, 1)
                    nc.vector.memset(smax[:, TPG - 1:TPG], 0.0).then_inc(carry_set, 1)

                    def slots(g, u):
                        load_slots(g, u, idx_ready, scattered)

                    def moments(g, u):
                        s = u % 2
                        wait(dve, gathered[u], laps(g, u, 32 * TPG))
                        wait(dve, v_eps_done, 2 * g)
                        for j, a in enumerate((xs, xd)):
                            for k in range(TPG):
                                n = nc.vector.bn_stats(st6[:, j, k, :], a[:, u, k, :])
                        n.then_inc(st_done, 1)
                        wait_apart(dve, (st_done, g + 1))
                        for j in range(2):
                            for k in range(TPG):
                                n = nc.vector.bn_aggr(mv[:, j, k, :], st6[:, j, k, :])
                        n.then_inc(mv_done, 1)
                        wait(dve, mv_done, g + 1)
                        wait(dve, h_done, (g - 1) * 2 * TPG)
                        nc.vector.tensor_scalar(neg_mean[:, s, :, :], mv[:, :, :, 0], -1.0, None,
                                                ALU.mult).then_inc(mean_done, 1)
                        wait(dve, rs_in_done, g)
                        nc.vector.tensor_scalar(var_eps[:, :, :], mv[:, :, :, 1], LN_EPS, None,
                                                ALU.add).then_inc(v_eps_done, 1)
                        wait(dve, rs_done, g - 1)
                        wait(dve, aug_done, g - 1)
                        nc.vector.tensor_scalar(rs_in[:, s, 2, :], mv[:, 0, :, 1], LN_EPS, None,
                                                ALU.add).then_inc(v_eps_done, 1)

                    def products(g, u):
                        s = u % 2
                        wait(dve, half_done, g - 1)
                        for k in range(TPG):
                            wait(dve, h_done, g * 2 * TPG + 2 * k + 2)
                            wait(dve, dot_done, g * TPG + k)
                            nc.vector.tensor_tensor_reduce(junk_v[:, :], hs[:, s, k, 0:D], hd[:, s, k, :], 1.0, 0.0,
                                                           ALU.mult, ALU.add,
                                                           accum_out=dot[:, s, k:k + 1]).then_inc(dot_done, 1)
                        wait(dve, sq_done, (g + 1) * 2 * TPG)
                        wait(dve, v_eps_done, 2 * g + 2)
                        nc.vector.scalar_tensor_tensor(rs_in[:, s, 0:2, :], var_eps[:, :, :], NORM_EPS * NORM_EPS,
                                                       sq[:, s, :, :], ALU.mult, ALU.max).then_inc(rs_in_done, 1)

                    def maxima(g, u):
                        s = u % 2
                        wait(dve, rs_done, g + 1)
                        wait(dve, dot_done, (g + 1) * TPG)
                        wait(dve, score_done, g)
                        nc.vector.scalar_tensor_tensor(half[:, :], dot[:, s, :], params[:, 6:7], rs[:, s, 0, :],
                                                       ALU.mult, ALU.mult).then_inc(half_done, 1)
                        wait(dve, half_done, g + 1)
                        wait(dve, erow_done, g - 1)
                        nc.vector.tensor_tensor(score[:, s, :], half[:, :], rs[:, s, 1, :],
                                                ALU.mult).then_inc(score_done, 1)
                        nc.vector.tensor_tensor(hs[:, s, :, D], rs_in[:, s, 2, :], rs[:, s, 2, :],
                                                ALU.mult).then_inc(aug_done, 1)
                        wait(dve, score_done, g + 1)
                        wait(dve, pw_done, g * TPG)
                        nc.vector.tensor_copy(ev[:, :, 0], score[:, s, :]).then_inc(ev_set, 1)
                        wait(dve, drow_done, g + 1)
                        wait(dve, max_done, g * TPG)
                        for k in range(TPG):
                            nc.vector.tensor_scalar(pen[:, k, :], D_ps[s][:, k * P:(k + 1) * P],
                                                    slot_f[:, u, 0, k:k + 1], LOWEST, ALU.not_equal,
                                                    ALU.mult).then_inc(pen_done, 1)
                        wait(dve, erow_done, g + 1)
                        wait(dve, ev_set, g + 1)
                        for k in range(TPG):
                            wait(dve, cm_done, g * TPG + k + 1)
                            nc.vector.tensor_scalar(ev[:, k, 1:2], M_ps[:, k:k + 1], slot_f[:, u, 1, k:k + 1], None,
                                                    ALU.add).then_inc(v_done, 1)
                            wait_apart(dve, (v_done, g * TPG + k + 1), (pen_done, g * TPG + k + 1),
                                       (ev_done, (g - 1) * TPG + k + 1), (cm_done, (g - 1) * TPG + k + 2))
                            nc.vector.tensor_tensor_reduce(pen[:, k, :], pen[:, k, :], E_ps[s][:, k * P:(k + 1) * P],
                                                           1.0, ev[:, k, 1:2], ALU.add, ALU.max,
                                                           accum_out=smax[:, k:k + 1]).then_inc(max_done, 1)
                            wait(dve, max_done, g * TPG + k + 1)
                            nc.vector.tensor_scalar(ev[:, k, :], ev[:, k, :], smax[:, k:k + 1], None,
                                                    ALU.subtract).then_inc(ev_done, 1)

                    def sums(g, u):
                        s = u % 2
                        wait(dve, pw_done, (g + 1) * TPG)
                        wait(dve, wsel_done, g * TPG)
                        nc.vector.tensor_tensor(p_rstd[:, :], pw[:, s, :, 0], rs[:, s, 2, :],
                                                ALU.mult).then_inc(p_rstd_done, 1)
                        wait(dve, p_rstd_done, g + 1)
                        for k in range(TPG):
                            wait(dve, u_done, (g - 1) * TPG + k + 1)
                            nc.vector.tensor_scalar(wsel[:, k, :], D_ps[s][:, k * P:(k + 1) * P],
                                                    slot_f[:, u, 0, k:k + 1], p_rstd[:, k:k + 1], ALU.is_equal,
                                                    ALU.mult).then_inc(wsel_done, 1)
                        wait(dve, scattered[(u - 2) % RING], laps(g - 2, (u - 2) % RING, 16 * TPG))
                        for k in range(TPG):
                            wait(dve, cu_done, g * TPG + k + 1)
                            wait(dve, part_done, g * TPG + k + 1)
                            wait(dve, row_done, g * TPG + k - 1)
                            nc.vector.scalar_tensor_tensor(acc[:, k % 2, :], C_ps[:, 0:AUG], pw[:, s, k, 1:2],
                                                           part[:, k % 2, :], ALU.mult, ALU.add).then_inc(acc_done, 1)
                            wait(dve, acc_done, g * TPG + k + 1)
                            nc.vector.reciprocal(rden[:, k:k + 1], acc[:, k % 2, D:AUG]).then_inc(rden_done, 1)
                            wait(dve, rden_done, g * TPG + k + 1)
                            nc.vector.scalar_tensor_tensor(rows[:, s, k, :], acc[:, k % 2, 0:D], rden[:, k:k + 1],
                                                           xd[:, u, k, :], ALU.mult, ALU.add).then_inc(row_done, 1)
                    pipeline(dve, (slots, 2), (moments, 1), (maxima, 0), (products, 1), (sums, 0))

                @block.tensor
                def _(pe):
                    pe.wait_ge(carry_set, 2)

                    def dst_rows(g, u):
                        s = u % 2
                        wait(pe, idx_ready, g + 1)
                        wait(pe, wsel_done, (g - 1) * TPG)
                        for k in range(TPG):
                            n = nc.tensor.matmul(D_ps[s][:, k * P:(k + 1) * P],
                                                 slot_f[:, u, 0, k:k + 1].broadcast_to([P, P]), ident[:, :],
                                                 start=True, stop=True)
                        n.then_inc(drow_done, 1)

                    def score_rows(g, u):
                        s = u % 2
                        wait(pe, score_done, g + 1)
                        wait(pe, max_done, (g - 1) * TPG)
                        for k in range(TPG):
                            n = nc.tensor.matmul(E_ps[s][:, k * P:(k + 1) * P],
                                                 score[:, s, k:k + 1].broadcast_to([P, P]), ident[:, :],
                                                 start=True, stop=True)
                        n.then_inc(erow_done, 1)
                        for k in range(TPG):
                            wait(pe, max_done, g * TPG + k)
                            wait(pe, v_done, (g - 1) * TPG + k + 1)
                            before = (k - 1) % TPG
                            nc.tensor.matmul(M_ps[:, k:k + 1], pick_last[:, :], smax[:, before:before + 1], start=True,
                                             stop=True).then_inc(cm_done, 1)

                    def segment_sums(g, u):
                        s = u % 2
                        wait(pe, aug_done, g + 1)
                        for k in range(TPG):
                            wait(pe, wsel_done, g * TPG + k + 1)
                            wait(pe, h_done, g * 2 * TPG + 2 * k + 1)
                            wait(pe, part_done, g * TPG + k - 1)
                            nc.tensor.matmul(U_ps[k % 2][:, 0:AUG], wsel[:, k, :], hs[:, s, k, :], start=True,
                                             stop=True).then_inc(u_done, 1)
                            wait(pe, acc_done, g * TPG + k)
                            nc.tensor.matmul(C_ps[:, 0:AUG], pick_last[:, :], acc[:, (k - 1) % 2, :], start=True,
                                             stop=True).then_inc(cu_done, 1)
                    pipeline(pe, (dst_rows, 0), (score_rows, 0), (segment_sums, 0))

        def mlp_front(tag, gather_rows, side, w_sb, bias_col, y_dram):
            with ExitStack() as c1:
                def sb1(name, shape, dt=fp32):
                    return c1.enter_context(nc.sbuf_tensor(tag + name, shape, dt))

                def sem1(name):
                    return c1.enter_context(nc.semaphore(tag + name))
                xs = sb1("xs", [P, RING, TPG, D])
                sd = sb1("sd", [P, RING, TPG, D])
                hs = sb1("hs", [P, 2, TPG, D])
                hT = sb1("hT", [P, 2, GW])
                sT = sb1("sT", [P, 2, GW])
                yT = sb1("yT", [P, RING, GW])
                st6 = sb1("st6", [P, TPG, 6])
                mv = sb1("mv", [P, 2, TPG, 2])
                var_eps = sb1("var_eps", [P, 2, TPG])
                rstd = sb1("rstd", [P, 2, TPG])
                shift = sb1("shift", [P, 2, TPG])
                idx_ready = sem1("idx_ready")
                rows_in = [sem1(f"rows_in{u}") for u in range(RING)]
                side_in = [sem1(f"side_in{u}") for u in range(RING)]
                y_out = [sem1(f"y_out{u}") for u in range(RING)]
                st_done, mv_done, v_eps_done, rstd_done, shift_done = (
                    sem1(n) for n in ("st_done", "mv_done", "v_eps_done", "rstd_done", "shift_done"))
                h_done, hT_ps_done, sT_ps_done = sem1("h_done"), sem1("hT_ps_done"), sem1("sT_ps_done")
                hT_done, sT_done, y_ps_done, y_done, bn_done = (
                    sem1(n) for n in ("hT_done", "sT_done", "y_ps_done", "y_done", "bn_done"))
                row_dmas = TPG if gather_rows else 1

                with nc.Block() as block:
                    @block.sync
                    def _(sp):
                        def load_side(g, u):
                            wait_apart(sp, (sT_ps_done, g - RING + 1))
                            for a, b in row_moves(side, sd[:, u, :, :], g, True):
                                sp.dma_start(a, b).then_inc(side_in[u], 16)

                        def load_rows(g, u):
                            wait_apart(sp, (h_done, g - RING + 1))
                            for a, b in row_moves(x1, xs[:, u, :, :], g, True):
                                sp.dma_start(a, b).then_inc(rows_in[u], 16)

                        def store_y(g, u):
                            wait_apart(sp, (y_done, g + 1))
                            sp.dma_start(y_dram[:, bass.ds(g * GW, GW)], yT[:, u, :]).then_inc(y_out[u], 16)
                        if gather_rows:
                            pipeline(sp, (load_side, 2), (store_y, -1))
                        else:
                            pipeline(sp, (load_rows, 3), (load_side, 2), (store_y, -1))
                        for u in range(RING):
                            sp.wait_ge(y_out[u], 16 * len(range(u, G, RING)))

                    @block.gpsimd
                    def _(pool):
                        last_row = pool.to_reg(N - 1) if gather_rows else None

                        def gather(g, u):
                            wait_apart(pool, (idx_ready, g + 1), (h_done, g - RING + 1))
                            for k in range(TPG):
                                nc.gpsimd.indirect_dma_start(
                                    xs[:, u, k, :], None, x1,
                                    bass.IndirectOffsetOnAxis(ap=slot_i[:, u, 0, k:k + 1], axis=0),
                                    bounds_check=last_row, oob_is_err=False).then_inc(rows_in[u], 16)

                        def rsqrt(g, u):
                            wait(pool, v_eps_done, g + 1)
                            wait(pool, h_done, g - 1)
                            wait(pool, shift_done, g - 1)
                            nc.gpsimd.tensor_tensor(rstd[:, u % 2, :], var_eps[:, u % 2, :],
                                                    minus_half[:, 0:TPG], ALU.pow).then_inc(rstd_done, 1)
                        if gather_rows:
                            pipeline(pool, (gather, 3), (rsqrt, 2))
                        else:
                            pipeline(pool, (rsqrt, 2))

                    @block.scalar
                    def _(act):
                        def normalise(g, u):
                            wait(act, shift_done, g + 1)
                            wait(act, hT_ps_done, g - 1)
                            for k in range(TPG):
                                n = nc.scalar.activation(hs[:, u % 2, k, :], xs[:, u, k, :], ACT.Relu,
                                                         bias=shift[:, u % 2, k:k + 1],
                                                         scale=rstd[:, u % 2, k:k + 1])
                            n.then_inc(h_done, 1)

                        def copy_side(g, u):
                            wait(act, sT_ps_done, g + 1)
                            wait(act, y_ps_done, g - 1)
                            nc.scalar.copy(sT[:, u % 2, :], ps[2 + u % 2][:, :]).then_inc(sT_done, 1)

                        def add_bias(g, u):
                            wait(act, y_ps_done, g + 1)
                            wait(act, y_out[u], laps(g, u, 16) - 16)
                            wait(act, bn_done, g - RING + 1)
                            nc.scalar.activation(yT[:, u, :], ps[4 + u % 2][:, :], ACT.Identity,
                                                 bias=params[:, bias_col:bias_col + 1], scale=1.0).then_inc(y_done, 1)
                        pipeline(act, (normalise, 1), (copy_side, 1), (add_bias, 0))

                    @block.vector
                    def _(dve):
                        def slots(g, u):
                            wait(dve, rows_in[u], laps(g, u, 16 * TPG) - 16 * TPG)
                            load_slots(g, u, idx_ready)

                        def moments(g, u):
                            wait(dve, rows_in[u], laps(g, u, 16 * row_dmas)
                                 + (16 if is_tail(g) and not gather_rows else 0))
                            wait(dve, mv_done, g)
                            for k in range(TPG):
                                n = nc.vector.bn_stats(st6[:, k, :], xs[:, u, k, :])
                            n.then_inc(st_done, 1)
                            wait_apart(dve, (st_done, g + 1), (shift_done, g - 1))
                            for k in range(TPG):
                                n = nc.vector.bn_aggr(mv[:, u % 2, k, :], st6[:, k, :])
                            n.then_inc(mv_done, 1)
                            wait(dve, mv_done, g + 1)
                            wait(dve, rstd_done, g - 1)
                            nc.vector.tensor_scalar(var_eps[:, u % 2, :], mv[:, u % 2, :, 1], LN_EPS, None,
                                                    ALU.add).then_inc(v_eps_done, 1)

                        def shifts(g, u):
                            wait(dve, rstd_done, g + 1)
                            wait(dve, h_done, g - 1)
                            nc.vector.scalar_tensor_tensor(shift[:, u % 2, :], mv[:, u % 2, :, 0], -1.0,
                                                           rstd[:, u % 2, :], ALU.mult,
                                                           ALU.mult).then_inc(shift_done, 1)

                        def copy_h(g, u):
                            wait(dve, hT_ps_done, g + 1)
                            wait(dve, y_ps_done, g - 1)
                            nc.vector.tensor_copy(hT[:, u % 2, :], ps[u % 2][:, :]).then_inc(hT_done, 1)

                        def count_y(g, u):
                            wait(dve, y_done, g + 1)
                            n = TAIL if is_tail(g) else GW
                            nc.vector.bn_stats(bn_sum[:, bass.ds(g, 1), :].rearrange("p o c -> p (o c)"),
                                               yT[:, u, 0:n]).then_inc(bn_done, 1)
                        if gather_rows:
                            pipeline(dve, (slots, 3), (moments, 2), (shifts, 1), (copy_h, 0), (count_y, -1))
                        else:
                            pipeline(dve, (moments, 2), (shifts, 1), (copy_h, 0), (count_y, -1))

                    @block.tensor
                    def _(pe):
                        def turn_side(g, u):
                            wait(pe, side_in[u], laps(g, u, 16) + (16 if is_tail(g) else 0))
                            wait(pe, sT_done, g - 1)
                            for k in range(TPG):
                                n = nc.tensor.transpose(ps[2 + u % 2][:, k * P:(k + 1) * P], sd[:, u, k, :],
                                                        ident[:, :])
                            n.then_inc(sT_ps_done, 1)

                        def turn_h(g, u):
                            wait(pe, h_done, g + 1)
                            wait(pe, hT_done, g - 1)
                            for k in range(TPG):
                                n = nc.tensor.transpose(ps[u % 2][:, k * P:(k + 1) * P], hs[:, u % 2, k, :],
                                                        ident[:, :])
                            n.then_inc(hT_ps_done, 1)

                        def product(g, u):
                            wait(pe, hT_done, g + 1)
                            wait(pe, sT_done, g + 1)
                            wait(pe, y_done, g - 1)
                            nc.tensor.matmul(ps[4 + u % 2][:, :], w_sb[:, 0, :], hT[:, u % 2, :], start=True, stop=False)
                            nc.tensor.matmul(ps[4 + u % 2][:, :], w_sb[:, 1, :], sT[:, u % 2, :], start=False,
                                             stop=True).then_inc(y_ps_done, 1)
                        pipeline(pe, (turn_side, 1), (turn_h, 0), (product, 0))

        def bn_coefficients(pool, dve, var_ready, inv_ready, step, gamma_col, beta_col):
            if dve is None:
                pool.wait_ge(var_ready, 1)
                nc.gpsimd.tensor_scalar(bn_rstd[:, :], bn_mv[:, 1:2], BN_EPS, None, ALU.add).then_inc(inv_ready, 1)
                pool.wait_ge(inv_ready, 1)
                nc.gpsimd.tensor_tensor(bn_rstd[:, :], bn_rstd[:, :], minus_half[:, 0:1], ALU.pow).then_inc(inv_ready, 1)
                return
            nc.vector.bn_aggr(bn_mv[:, :], bn_sum[:, :, :].rearrange("p g c -> p (g c)")).then_inc(var_ready, 1)
            dve.wait_ge(var_ready, 1)
            dve.wait_ge(inv_ready, 2)
            nc.vector.tensor_tensor(bn_s[:, :], bn_rstd[:, :], params[:, gamma_col:gamma_col + 1], ALU.mult).then_inc(step, 1)
            dve.wait_ge(step, 1)
            nc.vector.tensor_tensor(bn_tmp[:, :], bn_mv[:, 0:1], bn_s[:, :], ALU.mult).then_inc(step, 1)
            dve.wait_ge(step, 2)
            nc.vector.tensor_tensor(bn_t[:, :], params[:, beta_col:beta_col + 1], bn_tmp[:, :],
                                    ALU.subtract).then_inc(step, 1)

        mlp_front("p2_", True, edge_attr, w1_sb, 0, y1)

        with ExitStack() as c1:
            def sb1(name, shape, dt=fp32):
                return c1.enter_context(nc.sbuf_tensor("p3_" + name, shape, dt))

            def sem1(name):
                return c1.enter_context(nc.semaphore("p3_" + name))
            yT = sb1("yT", [P, RING, GW])
            ex = sb1("ex", [P, 2, GW])
            rl = sb1("rl", [P, 2, GW])
            el = sb1("el", [P, 2, GW])
            h1 = sb1("h1", [P, 2, TPG, AUG])
            sel = sb1("sel", [P, 2, TPG, D])
            part = sb1("part", [P, 2, AUG])
            acc = sb1("acc", [P, 2, AUG])
            cnt = sb1("cnt", [P, TPG])
            rden = sb1("rden", [P, TPG])
            rows = sb1("rows", [P, 2, TPG, D])
            D_ps, T_ps, U_ps, C_ps = [ps[0], ps[1]], [ps[2], ps[3]], [ps[4], ps[5]], ps[6]
            init_set, bn_var, bn_inv, bn_step, idx_ready = (
                sem1(n) for n in ("init_set", "bn_var", "bn_inv", "bn_step", "idx_ready"))
            y_in = [sem1(f"y_in{u}") for u in range(RING)]
            scattered = [sem1(f"scattered{u}") for u in range(RING)]
            ex_done, rl_done, el_done, elT_done, h1_done = (
                sem1(n) for n in ("ex_done", "rl_done", "el_done", "elT_done", "h1_done"))
            drow_done, sel_done, u_done, part_done, cu_done = (
                sem1(n) for n in ("drow_done", "sel_done", "u_done", "part_done", "cu_done"))
            acc_done, cnt_done, rden_done, row_done = (
                sem1(n) for n in ("acc_done", "cnt_done", "rden_done", "row_done"))

            with nc.Block() as block:
                @block.sync
                def _(sp):
                    def load_y(g, u):
                        wait_apart(sp, (rl_done, g - RING + 1))
                        sp.dma_start(yT[:, u, :], y1[:, bass.ds(g * GW, GW)]).then_inc(y_in[u], 16)
                    pipeline(sp, (load_y, 3))

                @block.gpsimd
                def _(pool):
                    last_row = pool.to_reg(N - 1)
                    bn_coefficients(pool, None, bn_var, bn_inv, bn_step, 1, 2)

                    def scatter(g, u):
                        for k in range(TPG):
                            wait_apart(pool, (row_done, g * TPG + k + 1))
                            nc.gpsimd.indirect_dma_start(
                                agg, bass.IndirectOffsetOnAxis(ap=slot_i[:, u, 2, k:k + 1], axis=0),
                                rows[:, u % 2, k, :], None, bounds_check=last_row,
                                oob_is_err=False).then_inc(scattered[u], 16)
                    pipeline(pool, (scatter, 0))
                    for u in range(RING):
                        pool.wait_ge(scattered[u], 16 * TPG * len(range(u, G, RING)))

                @block.scalar
                def _(act):
                    act.wait_ge(bn_step, 3)

                    def branches(g, u):
                        wait(act, y_in[u], laps(g, u, 16))
                        wait(act, el_done, g - 1)
                        nc.scalar.activation(ex[:, u % 2, :], yT[:, u, :], ACT.Exp, bias=bn_t[:, :],
                                             scale=bn_s[:, :]).then_inc(ex_done, 1)
                        nc.scalar.activation(rl[:, u % 2, :], yT[:, u, :], ACT.Relu, bias=bn_t[:, :],
                                             scale=bn_s[:, :]).then_inc(rl_done, 1)

                    def edge_major(g, u):
                        wait(act, elT_done, g + 1)
                        wait(act, u_done, (g - 1) * TPG)
                        if isinstance(g, int) and g < 2:
                            wait(act, init_set, 2)
                        nc.scalar.activation(h1[:, u % 2, :, 0:D],
                                             T_ps[u % 2][:, :].rearrange("p (k f) -> p k f", k=TPG),
                                             ACT.Copy, bias=-1.0).then_inc(h1_done, 1)

                    def parts(g, u):
                        for k in range(TPG):
                            wait(act, u_done, g * TPG + k + 1)
                            wait(act, acc_done, g * TPG + k - 1)
                            nc.scalar.copy(part[:, k % 2, :], U_ps[k % 2][:, 0:AUG]).then_inc(part_done, 1)
                    pipeline(act, (branches, 2), (edge_major, 1), (parts, 0))

                @block.vector
                def _(dve):
                    bn_coefficients(None, dve, bn_var, bn_inv, bn_step, 1, 2)
                    nc.vector.memset(h1[:, :, :, D:AUG], 1.0).then_inc(init_set, 1)
                    nc.vector.memset(acc[:, (TPG - 1) % 2, :], 0.0).then_inc(init_set, 1)

                    def slots(g, u):
                        load_slots(g, u, idx_ready, scattered)

                    def join(g, u):
                        wait(dve, ex_done, g + 1)
                        wait(dve, rl_done, g + 1)
                        wait(dve, elT_done, g - 1)
                        nc.vector.scalar_tensor_tensor(el[:, u % 2, :], ex[:, u % 2, :], 1.0, rl[:, u % 2, :], ALU.min,
                                                       ALU.add).then_inc(el_done, 1)

                    def selectors(g, u):
                        wait(dve, drow_done, g + 1)
                        wait(dve, idx_ready, g + 1)
                        wait(dve, u_done, (g - 1) * TPG)
                        for k in range(TPG):
                            nc.vector.tensor_scalar(sel[:, u % 2, k, :], D_ps[u % 2][:, k * P:(k + 1) * P],
                                                    slot_f[:, u, 0, k:k + 1], None,
                                                    ALU.is_equal).then_inc(sel_done, 1)

                    def means(g, u):
                        wait(dve, scattered[(u - 2) % RING], laps(g - 2, (u - 2) % RING, 16 * TPG))
                        for k in range(TPG):
                            wait(dve, cu_done, g * TPG + k + 1)
                            wait(dve, part_done, g * TPG + k + 1)
                            wait(dve, row_done, g * TPG + k - 1)
                            nc.vector.scalar_tensor_tensor(acc[:, k % 2, :], C_ps[:, 0:AUG], slot_f[:, u, 2, k:k + 1],
                                                           part[:, k % 2, :], ALU.mult, ALU.add).then_inc(acc_done, 1)
                            wait(dve, acc_done, g * TPG + k + 1)
                            nc.vector.tensor_scalar(cnt[:, k:k + 1], acc[:, k % 2, D:AUG], 1.0, None,
                                                    ALU.max).then_inc(cnt_done, 1)
                            wait(dve, cnt_done, g * TPG + k + 1)
                            nc.vector.reciprocal(rden[:, k:k + 1], cnt[:, k:k + 1]).then_inc(rden_done, 1)
                            wait(dve, rden_done, g * TPG + k + 1)
                            nc.vector.tensor_scalar(rows[:, u % 2, k, :], acc[:, k % 2, 0:D], rden[:, k:k + 1], None,
                                                    ALU.mult).then_inc(row_done, 1)
                    pipeline(dve, (slots, 2), (join, 2), (selectors, 1), (means, 0))

                @block.tensor
                def _(pe):
                    pe.wait_ge(init_set, 2)

                    def dst_rows(g, u):
                        wait(pe, idx_ready, g + 1)
                        wait(pe, sel_done, (g - 1) * TPG)
                        for k in range(TPG):
                            n = nc.tensor.matmul(D_ps[u % 2][:, k * P:(k + 1) * P],
                                                 slot_f[:, u, 0, k:k + 1].broadcast_to([P, P]), ident[:, :],
                                                 start=True, stop=True)
                        n.then_inc(drow_done, 1)

                    def turn_el(g, u):
                        wait(pe, el_done, g + 1)
                        wait(pe, h1_done, g - 1)
                        for k in range(TPG):
                            n = nc.tensor.transpose(T_ps[u % 2][:, k * P:(k + 1) * P],
                                                    el[:, u % 2, k * P:(k + 1) * P], ident[:, :])
                        n.then_inc(elT_done, 1)

                    def segment_sums(g, u):
                        wait(pe, h1_done, g + 1)
                        for k in range(TPG):
                            wait(pe, sel_done, g * TPG + k + 1)
                            wait(pe, part_done, g * TPG + k - 1)
                            nc.tensor.matmul(U_ps[k % 2][:, 0:AUG], sel[:, u % 2, k, :], h1[:, u % 2, k, :], start=True,
                                             stop=True).then_inc(u_done, 1)
                            wait(pe, acc_done, g * TPG + k)
                            nc.tensor.matmul(C_ps[:, 0:AUG], pick_last[:, :], acc[:, (k - 1) % 2, :], start=True,
                                             stop=True).then_inc(cu_done, 1)
                    pipeline(pe, (dst_rows, 1), (turn_el, 1), (segment_sums, 0))

        mlp_front("p4_", False, agg, w2_sb, 3, y2)

        with ExitStack() as c1:
            def sb1(name, shape, dt=fp32):
                return c1.enter_context(nc.sbuf_tensor("p5_" + name, shape, dt))

            def sem1(name):
                return c1.enter_context(nc.semaphore("p5_" + name))
            yT = sb1("yT", [P, RING, GW])
            xr = sb1("xr", [P, RING, TPG, D])
            ex = sb1("ex", [P, 2, GW])
            rl = sb1("rl", [P, 2, GW])
            el = sb1("el", [P, 2, GW])
            res = sb1("res", [P, RING, TPG, D])
            bn_var, bn_inv, bn_step = sem1("bn_var"), sem1("bn_inv"), sem1("bn_step")
            y_in = [sem1(f"y_in{u}") for u in range(RING)]
            x_in = [sem1(f"x_in{u}") for u in range(RING)]
            stored = [sem1(f"stored{u}") for u in range(RING)]
            ex_done, rl_done, el_done, elT_done, res_done = (
                sem1(n) for n in ("ex_done", "rl_done", "el_done", "elT_done", "res_done"))

            with nc.Block() as block:
                @block.sync
                def _(sp):
                    def load(g, u):
                        wait_apart(sp, (rl_done, g - RING + 1))
                        sp.dma_start(yT[:, u, :], y2[:, bass.ds(g * GW, GW)]).then_inc(y_in[u], 16)
                        wait_apart(sp, (res_done, g - RING + 1))
                        for a, b in row_moves(x1, xr[:, u, :, :], g, True):
                            sp.dma_start(a, b).then_inc(x_in[u], 16)

                    def store(g, u):
                        wait_apart(sp, (res_done, g + 1))
                        for a, b in row_moves(out, res[:, u, :, :], g, False):
                            sp.dma_start(a, b).then_inc(stored[u], 16)
                    pipeline(sp, (load, 2), (store, -1))
                    for u in range(RING):
                        sp.wait_ge(stored[u], 16 * (len(range(u, G, RING)) + (1 if u == (G - 1) % RING else 0)))

                @block.gpsimd
                def _(pool):
                    bn_coefficients(pool, None, bn_var, bn_inv, bn_step, 4, 5)

                @block.scalar
                def _(act):
                    act.wait_ge(bn_step, 3)

                    def branches(g, u):
                        wait(act, y_in[u], laps(g, u, 16))
                        wait(act, el_done, g - 1)
                        nc.scalar.activation(ex[:, u % 2, :], yT[:, u, :], ACT.Exp, bias=bn_t[:, :],
                                             scale=bn_s[:, :]).then_inc(ex_done, 1)
                        nc.scalar.activation(rl[:, u % 2, :], yT[:, u, :], ACT.Relu, bias=bn_t[:, :],
                                             scale=bn_s[:, :]).then_inc(rl_done, 1)
                    pipeline(act, (branches, 1))

                @block.vector
                def _(dve):
                    bn_coefficients(None, dve, bn_var, bn_inv, bn_step, 4, 5)

                    def join(g, u):
                        wait(dve, ex_done, g + 1)
                        wait(dve, rl_done, g + 1)
                        wait(dve, elT_done, g - 1)
                        nc.vector.scalar_tensor_tensor(el[:, u % 2, :], ex[:, u % 2, :], 1.0, rl[:, u % 2, :], ALU.min,
                                                       ALU.add).then_inc(el_done, 1)

                    def residual(g, u):
                        wait(dve, elT_done, g + 1)
                        wait(dve, x_in[u], laps(g, u, 16) + (16 if is_tail(g) else 0))
                        wait(dve, stored[u], laps(g, u, 16) - 16)
                        nc.vector.scalar_tensor_tensor(res[:, u, :, :].rearrange("p k f -> p (k f)"), ps[u % 2][:, :],
                                                       -1.0, xr[:, u, :, :].rearrange("p k f -> p (k f)"), ALU.add,
                                                       ALU.add).then_inc(res_done, 1)
                    pipeline(dve, (join, 1), (residual, 0))

                @block.tensor
                def _(pe):
                    def turn_el(g, u):
                        wait(pe, el_done, g + 1)
                        wait(pe, res_done, g - 1)
                        for k in range(TPG):
                            n = nc.tensor.transpose(ps[u % 2][:, k * P:(k + 1) * P], el[:, u % 2, k * P:(k + 1) * P],
                                                    ident[:, :])
                        n.then_inc(elT_done, 1)
                    pipeline(pe, (turn_el, 1))


_INS = ["x", "src", "dst", "edge_attr_128", "L0_gnn_beta", "L1_gnn_W1", "L1_gnn_b1", "L1_gnn_g1", "L1_gnn_be1",
        "L1_gnn_W2", "L1_gnn_b2", "L1_gnn_g2", "L1_gnn_be2"]


def kernel(**inputs):
    import numpy as np
    import concourse.bacc as bacc
    from concourse.bass_utils import run_bass_kernel_spmd

    nc = bacc.Bacc("TRN2", target_bir_lowering=False, num_devices=1)
    arrays, args = {}, []
    for name in _INS:
        a = np.ascontiguousarray(inputs[name])
        arrays[f"in_{name}"] = a
        args.append(nc.dram_tensor(f"in_{name}", a.shape, mybir.dt.from_np(a.dtype), kind="ExternalInput").ap())
    shape = inputs["x"].shape
    args.append(nc.dram_tensor("out_x", shape, mybir.dt.float32, kind="ExternalOutput").ap())
    build_gnn(nc, *args)
    r = run_bass_kernel_spmd(nc, [arrays], core_ids=[0])
    return r.results[0]["out_x"]
```

```python
from contextlib import ExitStack

import concourse.bass as bass
from concourse import mybir

P = 128
TPG = 4
RING = 4
X1_PIECES = 8
ZERO_ROWS = 16
GW = P * TPG
FAR = float(2 ** 20)
LOWEST = -3.0e38
LN_EPS = 1e-5
BN_EPS = 1e-4
NORM_EPS = 1e-12


def build_gnn(nc, x, src, dst, edge_attr, beta, W1, b1, g1, be1, W2, b2, g2, be2, out):
    fp32, i32 = mybir.dt.float32, mybir.dt.int32
    ALU, ACT = mybir.AluOpType, mybir.ActivationFunctionType
    N, D = x.shape
    E = src.shape[0]
    assert D == P and E == N
    G = -(-N // GW)
    assert G >= 2 * RING + 4
    T = G * TPG
    TAIL = N - (G - 1) * GW
    TAIL_FULL, TAIL_REST = TAIL // P, TAIL % P
    TB = -(-T // P)
    AUG = D + 1

    ctx = ExitStack()
    with ctx:
        def sb(name, shape, dt=fp32):
            return ctx.enter_context(nc.sbuf_tensor(name, shape, dt))

        def sem(name):
            return ctx.enter_context(nc.semaphore(name))

        def dram(name, shape):
            return nc.dram_tensor(name, shape, fp32, kind="Internal").ap()

        x1 = dram("x1", [N, D])
        agg = dram("agg", [N, D])
        ea_sorted = dram("ea_sorted", [T * P, D])
        src_sorted = nc.dram_tensor("src_sorted", [T * P, 1], i32, kind="Internal").ap()
        dst_sorted = nc.dram_tensor("dst_sorted", [T * P, 1], i32, kind="Internal").ap()
        y1 = dram("y1", [P, G * GW])
        y2 = dram("y2", [P, G * GW])

        wait_carrier = sem("wait_carrier")
        ps = [ctx.enter_context(nc.psum_tensor(f"bank{i}", [P, GW], fp32)) for i in range(8)]

        ident = sb("ident", [P, P])
        pick_last = sb("pick_last", [P, P])
        shift_up = sb("shift_up", [P, P])
        wrap_up = sb("wrap_up", [P, P])
        minus_half = sb("minus_half", [P, 3 * TPG])
        earlier = sb("earlier", [P, P])
        ones_col = sb("ones_col", [P, 1])
        zeros = sb("zeros", [P, ZERO_ROWS * D])
        unsorted = sb("unsorted", [1, 1], i32)
        x1_init, agg_zero = sem("x1_init"), sem("agg_zero")
        edge_f = sb("edge_f", [P, G, 4, TPG])
        edge_i = sb("edge_i", [P, G, 3, TPG], i32)
        slot_f = sb("slot_f", [P, RING, 4, TPG])
        slot_i = sb("slot_i", [P, RING, 3, TPG], i32)
        w1_sb = sb("w1_sb", [P, 2, D])
        w2_sb = sb("w2_sb", [P, 2, D])
        params = sb("params", [P, 7])
        bn_sum = sb("bn_sum", [P, G, 6])
        bn_mv = sb("bn_mv", [P, 2])
        bn_s = sb("bn_s", [P, 1])
        bn_t = sb("bn_t", [P, 1])
        bn_tmp = sb("bn_tmp", [P, 1])
        bn_rstd = sb("bn_rstd", [P, 1])

        def pipeline(*parts):
            eng, parts = parts[0], parts[1:]

            def step(g, u):
                for part, ahead in parts:
                    j = g + ahead
                    if not isinstance(j, int) or 0 <= j < G:
                        part(j, (u + ahead) % RING)
            first, most, least = RING, max(a for _, a in parts), min(a for _, a in parts)
            stop = first + (G - 1 - most - first) // RING * RING
            for g in range(-most, first):
                step(g, g % RING)
            with eng.Fori(first // RING, stop // RING) as turn:
                for u in range(RING):
                    step(turn * RING + u, u)
            for g in range(stop, G - least):
                step(g, g % RING)

        def wait(eng, s, value):
            if not isinstance(value, int) or value > 0:
                eng.wait_ge(s, value)

        def wait_apart(eng, *waits):
            for s, v in waits:
                wait(eng, s, v)
            if any(not isinstance(v, int) for _, v in waits):
                eng.sem_inc(wait_carrier, 1)

        def is_tail(g):
            return isinstance(g, int) and g == G - 1

        def laps(g, u, per):
            return (g - u) * (per // RING) + per

        def load_slots(j, u, ready, sem_scattered=None):
            if sem_scattered is not None:
                wait(nc.vector, sem_scattered[u], laps(j, u, 16 * TPG) - 16 * TPG)
            nc.vector.tensor_copy(slot_f[:, u, :, :], edge_f[:, bass.ds(j, 1), :, :].rearrange("p o a k -> p (o a) k"))
            nc.vector.tensor_copy(slot_i[:, u, :, :],
                                  edge_i[:, bass.ds(j, 1), :, :].rearrange("p o a k -> p (o a) k")).then_inc(ready, 1)

        def row_moves(dram_rows, tile, g, load):
            if is_tail(g):
                r0 = g * GW
                full = dram_rows[r0:r0 + TAIL_FULL * P, :].rearrange("(k p) f -> p k f", p=P)
                rest = dram_rows[r0 + TAIL_FULL * P:N, :]
                pieces = [(full, tile[:, 0:TAIL_FULL, :]), (rest, tile[0:TAIL_REST, TAIL_FULL, :])]
            else:
                pieces = [(dram_rows[bass.ds(g * GW, GW), :].rearrange("(k p) f -> p k f", p=P), tile)]
            return [(b, a) if load else (a, b) for a, b in pieces]

        def load_columns(sp, pieces, done):
            for to, frm in pieces:
                sp.dma_start(to, frm).then_inc(done, 16)

        def index_pieces(raw_i, lists, count):
            pieces = []
            for j, idx in enumerate(lists):
                for b in range(TB):
                    r0, r1 = b * P, min((b + 1) * P, count // P)
                    if r1 > r0:
                        pieces.append((raw_i[0:r1 - r0, j, b, :], idx[r0 * P:r1 * P].rearrange("(r c) -> r c", c=P)))
                r = count // P
                if count % P:
                    pieces.append((raw_i[r % P:r % P + 1, j, r // P, 0:count % P],
                                   idx[r * P:count].rearrange("(r c) -> r c", r=1)))
            return pieces

        with ExitStack() as c1:
            def sb1(name, shape, dt=fp32):
                return c1.enter_context(nc.sbuf_tensor(name, shape, dt))

            def sem1(name):
                return c1.enter_context(nc.semaphore(name))
            raw_i = sb1("raw_i", [P, 2, TB, P], i32)
            raw_f = sb1("raw_f", [P, 2, TB, P])
            src_f = sb1("src_f", [P, TB * P])
            dst_f = sb1("dst_f", [P, TB * P])
            falls = sb1("falls", [P, TB * P])
            fall = sb1("fall", [P, 1])
            unsorted_here = sb1("unsorted_here", [1, 1])

            raw_set, raw_in = sem1("raw_set"), sem1("raw_in")
            const_set, const_ready = sem1("const_set"), sem1("const_ready")
            small_in, zeros_set = sem1("small_in"), sem1("zeros_set")
            as_float, turned, placed = sem1("as_float"), sem1("turned"), sem1("placed")
            neigh, flag_step, fall_sum = sem1("neigh"), sem1("flag_step"), sem1("fall_sum")

            def next_destinations(pe):
                nc.tensor.matmul(ps[3][:, 0:T], shift_up[:, :], dst_f[:, 0:T], start=True, stop=False)
                return nc.tensor.matmul(ps[3][:, 0:T], wrap_up[:, :], dst_f[:, 1:T + 1], start=False, stop=True)

            def turn_lists(pe):
                for j in range(2):
                    for b in range(TB):
                        t = nc.tensor.transpose(ps[j][:, b * P:(b + 1) * P], raw_f[:, j, b, :], ident[:, :])
                return t

            first_pieces = index_pieces(raw_i, (src, dst), E)
            with nc.Block() as block:
                @block.sync
                def _(sp):
                    sp.wait_ge(raw_set, 2)
                    load_columns(sp, first_pieces, raw_in)
                    for j, v in enumerate((b1, g1, be1, b2, g2, be2)):
                        sp.dma_start(params[:, j:j + 1], v.rearrange("(p o) -> p o", o=1)).then_inc(small_in, 16)
                    sp.dma_start(params[:, 6:7],
                                 beta.rearrange("(p o) -> p o", p=1).broadcast_to([P, 1])).then_inc(small_in, 16)
                    sp.dma_start(w1_sb[:, :, :], W1.rearrange("(h k) c -> k h c", h=2)).then_inc(small_in, 16)
                    sp.dma_start(w2_sb[:, :, :], W2.rearrange("(h k) c -> k h c", h=2)).then_inc(small_in, 16)
                    step = -(-N // X1_PIECES)
                    for a in range(0, N, step):
                        b = min(N, a + step)
                        sp.dma_start(x1[a:b, :], x[a:b, :]).then_inc(x1_init, 16)
                    sp.wait_ge(small_in, 9 * 16)

                @block.gpsimd
                def _(pool):
                    nc.gpsimd.memset(raw_i[:, 0, :, :], 0).then_inc(raw_set, 1)
                    nc.gpsimd.memset(raw_i[:, 1, :, :], int(FAR)).then_inc(raw_set, 1)
                    nc.gpsimd.memset(minus_half[:, :], -0.5)
                    for m in (ident, pick_last, shift_up, wrap_up):
                        nc.gpsimd.memset(m[:, :], 0.0).then_inc(const_set, 1)
                    nc.gpsimd.memset(earlier[:, :], 1.0).then_inc(const_set, 1)
                    pool.wait_ge(const_set, 5)
                    for m, base in ((ident, 0), (shift_up, -1)):
                        nc.gpsimd.affine_select(out=m[:, :], in_=m[:, :], compare_op=ALU.not_equal, fill=1.0,
                                                base=base, pattern=[[-1, P]],
                                                channel_multiplier=1).then_inc(const_ready, 1)
                    nc.gpsimd.affine_select(out=pick_last[:, :], in_=pick_last[:, :], compare_op=ALU.not_equal,
                                            fill=1.0, base=-(P - 1), pattern=[[0, P]],
                                            channel_multiplier=1).then_inc(const_ready, 1)
                    nc.gpsimd.affine_select(out=wrap_up[:, P - 1:P], in_=wrap_up[:, P - 1:P],
                                            compare_op=ALU.not_equal, fill=1.0, base=0, pattern=[[0, 1]],
                                            channel_multiplier=1).then_inc(const_ready, 1)
                    nc.gpsimd.affine_select(out=earlier[:, :], in_=earlier[:, :], compare_op=ALU.is_gt, fill=0.0,
                                            base=0, pattern=[[-1, P]],
                                            channel_multiplier=1).then_inc(const_ready, 1)

                @block.vector
                def _(dve):
                    nc.vector.memset(zeros[:, :], 0.0)
                    nc.vector.memset(ones_col[:, :], 1.0).then_inc(zeros_set, 1)
                    dve.wait_ge(raw_in, 16 * len(first_pieces))
                    nc.vector.tensor_copy(raw_f[:, :, :, :], raw_i[:, :, :, :]).then_inc(as_float, 1)
                    dve.wait_ge(turned, 1)
                    nc.vector.tensor_copy(src_f[:, :], ps[0][:, 0:TB * P]).then_inc(placed, 1)
                    nc.vector.tensor_copy(dst_f[:, :], ps[1][:, 0:TB * P]).then_inc(placed, 1)
                    dve.wait_ge(neigh, 1)
                    nc.vector.tensor_tensor(falls[:, 0:T], dst_f[:, 0:T], ps[3][:, 0:T], ALU.is_gt).then_inc(flag_step, 1)
                    dve.wait_ge(flag_step, 1)
                    nc.vector.reduce_max(fall[:, :], falls[:, 0:T], mybir.AxisListType.X).then_inc(flag_step, 1)
                    dve.wait_ge(fall_sum, 1)
                    nc.vector.tensor_scalar(unsorted_here[:, :], ps[4][0:1, 0:1], 1.0, None, ALU.min).then_inc(flag_step, 1)
                    dve.wait_ge(flag_step, 3)
                    nc.vector.tensor_copy(unsorted[:, :], unsorted_here[:, :])

                @block.tensor
                def _(pe):
                    pe.wait_ge(const_ready, 5)
                    pe.wait_ge(as_float, 1)
                    turn_lists(pe).then_inc(turned, 1)
                    pe.wait_ge(placed, 2)
                    next_destinations(pe).then_inc(neigh, 1)
                    pe.wait_ge(flag_step, 2)
                    pe.wait_ge(zeros_set, 1)
                    nc.tensor.matmul(ps[4][0:1, 0:1], fall[:, :], ones_col[:, :], start=True,
                                     stop=True).then_inc(fall_sum, 1)

            with ExitStack() as c2:
                def sb2(name, shape, dt=fp32):
                    return c2.enter_context(nc.sbuf_tensor(name, shape, dt))

                def sem2(name):
                    return sem("sort_" + name)
                all_dst = sb2("all_dst", [P, T * P], mybir.dt.uint16)
                counted = sb2("counted", [P, T * P], mybir.dt.uint8)
                tied = sb2("tied", [P, P])
                col = sb2("col", [P, 1])
                limit = sb2("limit", [P, 1])
                below = sb2("below", [P, 1])
                ties = sb2("ties", [P, 1])
                rank = sb2("rank", [P, 1], i32)
                src_i = sb2("src_i", [P, 1], i32)
                dst_i = sb2("dst_i", [P, 1], i32)
                ea_row = sb2("ea_row", [P, D])
                col_set, col_row, row_set = sem2("col_set"), sem2("col_row"), sem2("row_set")
                limit_set, below_set, ties_set, rank_set, lowered = (
                    sem2(n) for n in ("limit_set", "below_set", "ties_set", "rank_set", "lowered"))
                ea_in, list_out, ea_out = sem2("ea_in"), sem2("list_out"), sem2("ea_out")
                reloaded, sorted_float, sorted_turned = sem2("reloaded"), sem2("float"), sem2("turned")
                again = index_pieces(raw_i, (src_sorted.rearrange("r o -> (r o)"),
                                             dst_sorted.rearrange("r o -> (r o)")), T * P)
                FULL = E // P

                def over_tiles(eng, tile, whole):
                    tile(0)
                    with eng.Fori(1, whole) as t:
                        tile(t)
                    for t in range(whole, T):
                        tile(t)

                def when_unsorted(eng, body):
                    flag = eng.value_load(unsorted[0:1, 0:1], min_val=0, max_val=1)
                    with eng.If(flag > 0):
                        body()
                    eng.end_ifs()

                with nc.Block() as block:
                    @block.sync
                    def _(sp):
                        def tile(t):
                            wait_apart(sp, (ea_out, t * 16))
                            rows = E - t * P if isinstance(t, int) and t >= FULL else P
                            if rows > 0:
                                sp.dma_start(ea_row[0:rows, :], edge_attr[bass.ds(t * P, rows), :]).then_inc(ea_in, 16)
                            else:
                                sp.sem_inc(ea_in, 16)

                        def body():
                            over_tiles(sp, tile, FULL)
                            sp.wait_ge(list_out, 2 * 16 * T)
                            load_columns(sp, again, reloaded)
                        when_unsorted(sp, body)

                    @block.gpsimd
                    def _(pool):
                        def tile(t):
                            for frm, to in ((src_i, src_sorted), (dst_i, dst_sorted), (ea_row, ea_sorted)):
                                if frm is src_i:
                                    wait_apart(pool, (rank_set, t + 1))
                                if frm is ea_row:
                                    wait_apart(pool, (ea_in, t * 16 + 16))
                                nc.gpsimd.indirect_dma_start(
                                    to, bass.IndirectOffsetOnAxis(ap=rank[:, 0:1], axis=0), frm[:, :], None,
                                    bounds_check=T * P - 1, oob_is_err=False
                                ).then_inc(ea_out if frm is ea_row else list_out, 16)

                        def body():
                            over_tiles(pool, tile, FULL)
                            pool.wait_ge(ea_out, 16 * T)
                        when_unsorted(pool, body)

                    @block.vector
                    def _(dve):
                        def spread(t):
                            wait(dve, col_row, t)
                            nc.vector.tensor_copy(col[:, :], dst_f[:, bass.ds(t, 1)]).then_inc(col_set, 1)
                            wait(dve, col_row, t + 1)
                            nc.vector.tensor_scalar(all_dst[:, bass.ds(t * P, P)], ps[0][:, 0:P], 1.0, 65535.0,
                                                    ALU.add, ALU.min).then_inc(row_set, 1)

                        def rank_tile(t):
                            own = all_dst[:, bass.ds(t * P, P)]
                            nc.vector.tensor_scalar(limit[:, :], dst_f[:, bass.ds(t, 1)], 1.0, 65535.0, ALU.add,
                                                    ALU.min).then_inc(limit_set, 1)
                            wait(dve, limit_set, t + 1)
                            wait(dve, lowered, t)
                            nc.vector.tensor_scalar(counted[:, :], all_dst[:, :], limit[:, :], 0.0, ALU.is_lt, ALU.add,
                                                    accum_out=below[:, :]).then_inc(below_set, 1)
                            nc.vector.scalar_tensor_tensor(tied[:, :], own, limit[:, :], earlier[:, :], ALU.is_equal,
                                                           ALU.mult, accum_out=ties[:, :]).then_inc(ties_set, 1)
                            wait(dve, below_set, t + 1)
                            wait(dve, ties_set, t + 1)
                            wait(dve, list_out, t * 32)
                            wait(dve, ea_out, t * 16)
                            nc.vector.tensor_copy(src_i[:, :], src_f[:, bass.ds(t, 1)])
                            nc.vector.tensor_copy(dst_i[:, :], dst_f[:, bass.ds(t, 1)])
                            nc.vector.tensor_tensor(rank[:, :], below[:, :], ties[:, :], ALU.add).then_inc(rank_set, 1)
                            nc.vector.tensor_scalar(own, own, 1.0, None, ALU.subtract).then_inc(lowered, 1)
                            wait(dve, lowered, t + 1)

                        def body():
                            over_tiles(dve, spread, T)
                            dve.wait_ge(row_set, T)
                            over_tiles(dve, rank_tile, T)
                            dve.wait_ge(reloaded, 16 * len(again))
                            nc.vector.tensor_copy(raw_f[:, :, :, :], raw_i[:, :, :, :]).then_inc(sorted_float, 1)
                            dve.wait_ge(sorted_turned, 1)
                            nc.vector.tensor_copy(src_f[:, :], ps[0][:, 0:TB * P])
                            nc.vector.tensor_copy(dst_f[:, :], ps[1][:, 0:TB * P])
                        when_unsorted(dve, body)

                    @block.tensor
                    def _(pe):
                        def spread(t):
                            wait(pe, col_set, t + 1)
                            wait(pe, row_set, t)
                            nc.tensor.matmul(ps[0][:, 0:P], col[:, 0:1].broadcast_to([P, P]), ident[:, :], start=True,
                                             stop=True).then_inc(col_row, 1)

                        def body():
                            over_tiles(pe, spread, T)
                            pe.wait_ge(sorted_float, 1)
                            pe.wait_ge(row_set, T)
                            turn_lists(pe).then_inc(sorted_turned, 1)
                        when_unsorted(pe, body)

            same = sb1("same", [P, TB * P])
            last = sb1("last", [P, TB * P])
            far = sb1("far", [P, TB * P])
            table_neigh, table_step, reach = sem1("table_neigh"), sem1("table_step"), sem1("reach")
            with nc.Block() as block:
                @block.vector
                def _(dve):
                    dst_g = dst_f[:, 0:T].rearrange("p (g k) -> p g k", k=TPG)
                    nc.vector.tensor_copy(edge_i[:, :, 0, :], src_f[:, 0:T].rearrange("p (g k) -> p g k", k=TPG))
                    nc.vector.tensor_copy(edge_f[:, :, 0, :], dst_g)
                    nc.vector.tensor_scalar(edge_i[:, :, 1, :], dst_g, float(N - 1), None, ALU.min)
                    dve.wait_ge(table_neigh, 1)
                    nc.vector.memset(same[:, 0:1], 0.0)
                    nc.vector.tensor_tensor(same[:, 1:T], dst_f[:, 1:T], ps[2][:, 0:T - 1],
                                            ALU.is_equal).then_inc(table_step, 1)
                    nc.vector.tensor_tensor(last[:, 0:T], dst_f[:, 0:T], ps[3][:, 0:T],
                                            ALU.is_equal).then_inc(table_step, 1)
                    dve.wait_ge(table_step, 2)
                    same_g = same[:, 0:T].rearrange("p (g k) -> p g k", k=TPG)
                    nc.vector.tensor_copy(edge_f[:, :, 2, :], same_g)
                    nc.vector.tensor_scalar(edge_f[:, :, 1, :], same_g, 1.0, -LOWEST, ALU.subtract, ALU.mult)
                    nc.vector.scalar_tensor_tensor(far[:, 0:T], last[:, 0:T], FAR, dst_f[:, 0:T],
                                                   ALU.mult, ALU.add).then_inc(table_step, 1)
                    dve.wait_ge(table_step, 3)
                    nc.vector.tensor_copy(edge_i[:, :, 2, :], far[:, 0:T].rearrange("p (g k) -> p g k", k=TPG))
                    dve.wait_ge(reach, 1)
                    nc.vector.tensor_scalar(edge_f[:, :, 3, :], ps[4][:, 0:T].rearrange("p (g k) -> p g k", k=TPG),
                                            1.0, -LOWEST, ALU.subtract, ALU.mult)

                @block.tensor
                def _(pe):
                    nc.tensor.matmul(ps[2][:, 0:T], pick_last[:, :], dst_f[:, 0:T], start=True, stop=True)
                    next_destinations(pe).then_inc(table_neigh, 1)
                    pe.wait_ge(table_step, 2)
                    nc.tensor.matmul(ps[4][:, 0:T], pick_last[:, :], same[:, 0:T], start=True,
                                     stop=True).then_inc(reach, 1)

        zero_pieces = []
        for a in range(0, N, ZERO_ROWS * P):
            rest = min(N - a, ZERO_ROWS * P)
            q = max(n for n in range(1, P + 1) if rest % n == 0 and rest // n <= ZERO_ROWS)
            zero_pieces.append((agg[a:a + rest, :].rearrange("(p r) f -> p (r f)", p=q), q, rest // q * D))

        with ExitStack() as c1:
            def sb1(name, shape, dt=fp32):
                return c1.enter_context(nc.sbuf_tensor("p1_" + name, shape, dt))

            def sem1(name):
                return c1.enter_context(nc.semaphore("p1_" + name))
            xs = sb1("xs", [P, RING, TPG, D])
            xd = sb1("xd", [P, RING, TPG, D])
            hs = sb1("hs", [P, 2, TPG, AUG])
            hd = sb1("hd", [P, 2, TPG, D])
            junk_a = sb1("junk_a", [P, D])
            junk_v = sb1("junk_v", [P, D])
            st6 = sb1("st6", [P, 2, TPG, 6])
            mv = sb1("mv", [P, 2, TPG, 2])
            neg_mean = sb1("neg_mean", [P, 2, 2, TPG])
            var_eps = sb1("var_eps", [P, 2, TPG])
            sq = sb1("sq", [P, 2, 2, TPG])
            dot = sb1("dot", [P, 2, TPG])
            rs_in = sb1("rs_in", [P, 2, 3, TPG])
            rs = sb1("rs", [P, 2, 3, TPG])
            half = sb1("half", [P, TPG])
            score = sb1("score", [P, 2, TPG])
            pen = sb1("pen", [P, TPG, D])
            smax = sb1("smax", [P, TPG])
            ev = sb1("ev", [P, TPG, 2])
            pw = sb1("pw", [P, 2, TPG, 2])
            p_rstd = sb1("p_rstd", [P, TPG])
            wsel = sb1("wsel", [P, TPG, D])
            part = sb1("part", [P, 2, AUG])
            acc = sb1("acc", [P, 2, AUG])
            rden = sb1("rden", [P, TPG])
            rows = sb1("rows", [P, 2, TPG, D])
            D_ps, E_ps, U_ps = [ps[0], ps[1]], [ps[2], ps[3]], [ps[4], ps[5]]
            C_ps, M_ps = ps[6], ps[7]

            carry_set, idx_ready = sem1("carry_set"), sem1("idx_ready")
            gathered = [sem1(f"gathered{u}") for u in range(RING)]
            scattered = [sem1(f"scattered{u}") for u in range(RING)]
            st_done, mv_done, mean_done, v_eps_done = (sem1(n) for n in ("st_done", "mv_done", "mean_done", "v_eps_done"))
            h_done, sq_done, dot_done = sem1("h_done"), sem1("sq_done"), sem1("dot_done")
            rs_in_done, rs_done, half_done, score_done = (sem1(n) for n in ("rs_in_done", "rs_done", "half_done", "score_done"))
            aug_done = sem1("aug_done")
            drow_done, erow_done, pen_done = sem1("drow_done"), sem1("erow_done"), sem1("pen_done")
            ev_set, cm_done, v_done, max_done, ev_done = (sem1(n) for n in ("ev_set", "cm_done", "v_done", "max_done", "ev_done"))
            pw_done, p_rstd_done, wsel_done = sem1("pw_done"), sem1("p_rstd_done"), sem1("wsel_done")
            u_done, part_done, cu_done, acc_done = sem1("u_done"), sem1("part_done"), sem1("cu_done"), sem1("acc_done")
            rden_done, row_done = sem1("rden_done"), sem1("row_done")

            with nc.Block() as block:
                @block.sync
                def _(sp):
                    for to, q, n in zero_pieces:
                        sp.dma_start(to, zeros[0:q, 0:n]).then_inc(agg_zero, 16)

                @block.gpsimd
                def _(pool):
                    last_row = pool.to_reg(N - 1)

                    def gather(g, u):
                        wait_apart(pool, (idx_ready, g + 1), (row_done, (g - RING + 1) * TPG))
                        for k in range(TPG):
                            for rows_to, col in ((xs, 0), (xd, 1)):
                                nc.gpsimd.indirect_dma_start(
                                    rows_to[:, u, k, :], None, x,
                                    bass.IndirectOffsetOnAxis(ap=slot_i[:, u, col, k:k + 1], axis=0),
                                    bounds_check=last_row, oob_is_err=False).then_inc(gathered[u], 16)

                    def rsqrt(g, u):
                        wait(pool, rs_in_done, g + 1)
                        wait(pool, wsel_done, (g - 1) * TPG)
                        nc.gpsimd.tensor_tensor(rs[:, u % 2, :, :], rs_in[:, u % 2, :, :],
                                                minus_half[:, :].rearrange("p (a k) -> p a k", k=TPG),
                                                ALU.pow).then_inc(rs_done, 1)

                    def scatter(g, u):
                        if isinstance(g, int) and g == 0:
                            pool.wait_ge(x1_init, 16 * X1_PIECES)
                        for k in range(TPG):
                            wait_apart(pool, (row_done, g * TPG + k + 1))
                            nc.gpsimd.indirect_dma_start(
                                x1, bass.IndirectOffsetOnAxis(ap=slot_i[:, u, 2, k:k + 1], axis=0),
                                rows[:, u % 2, k, :], None, bounds_check=last_row,
                                oob_is_err=False).then_inc(scattered[u], 16)
                    pipeline(pool, (rsqrt, 0), (gather, 2), (scatter, -1))
                    for u in range(RING):
                        pool.wait_ge(scattered[u], 16 * TPG * len(range(u, G, RING)))

                @block.scalar
                def _(act):
                    def center(g, u):
                        s = u % 2
                        wait(act, mean_done, g + 1)
                        wait(act, u_done, (g - 1) * TPG)
                        wait(act, dot_done, (g - 1) * TPG)
                        wait(act, rs_in_done, g - 1)
                        for k in range(TPG):
                            for j, (a, h) in enumerate(((xs, hs), (xd, hd))):
                                nc.scalar.activation(h[:, s, k, 0:D], a[:, u, k, :], ACT.Relu,
                                                     bias=neg_mean[:, s, j, k:k + 1]).then_inc(h_done, 1)
                        for k in range(TPG):
                            for j, h in enumerate((hs, hd)):
                                wait(act, h_done, g * 2 * TPG + 2 * k + j + 1)
                                wait(act, sq_done, g * 2 * TPG + 2 * k + j)
                                nc.scalar.activation(junk_a[:, :], h[:, s, k, 0:D], ACT.Square,
                                                     accum_out=sq[:, s, j, k:k + 1]).then_inc(sq_done, 1)

                    def weigh(g, u):
                        s = u % 2
                        wait(act, acc_done, (g - 1) * TPG)
                        for k in range(TPG):
                            wait(act, ev_done, g * TPG + k + 1)
                            nc.scalar.activation(pw[:, s, k, :], ev[:, k, :], ACT.Exp).then_inc(pw_done, 1)
                        for k in range(TPG):
                            wait(act, u_done, g * TPG + k + 1)
                            wait(act, acc_done, g * TPG + k - 1)
                            nc.scalar.copy(part[:, k % 2, :], U_ps[k % 2][:, 0:AUG]).then_inc(part_done, 1)
                    pipeline(act, (center, 1), (weigh, 0))

                @block.vector
                def _(dve):
                    nc.vector.memset(acc[:, (TPG - 1) % 2, :], 0.0).then_inc(carry_set, 1)
                    nc.vector.memset(smax[:, TPG - 1:TPG], 0.0).then_inc(carry_set, 1)

                    def slots(g, u):
                        load_slots(g, u, idx_ready, scattered)

                    def moments(g, u):
                        s = u % 2
                        wait(dve, gathered[u], laps(g, u, 32 * TPG))
                        wait(dve, v_eps_done, 2 * g)
                        for j, a in enumerate((xs, xd)):
                            for k in range(TPG):
                                n = nc.vector.bn_stats(st6[:, j, k, :], a[:, u, k, :])
                        n.then_inc(st_done, 1)
                        wait_apart(dve, (st_done, g + 1))
                        for j in range(2):
                            for k in range(TPG):
                                n = nc.vector.bn_aggr(mv[:, j, k, :], st6[:, j, k, :])
                        n.then_inc(mv_done, 1)
                        wait(dve, mv_done, g + 1)
                        wait(dve, h_done, (g - 1) * 2 * TPG)
                        nc.vector.tensor_scalar(neg_mean[:, s, :, :], mv[:, :, :, 0], -1.0, None,
                                                ALU.mult).then_inc(mean_done, 1)
                        wait(dve, rs_in_done, g)
                        nc.vector.tensor_scalar(var_eps[:, :, :], mv[:, :, :, 1], LN_EPS, None,
                                                ALU.add).then_inc(v_eps_done, 1)
                        wait(dve, rs_done, g - 1)
                        wait(dve, aug_done, g - 1)
                        nc.vector.tensor_scalar(rs_in[:, s, 2, :], mv[:, 0, :, 1], LN_EPS, None,
                                                ALU.add).then_inc(v_eps_done, 1)

                    def products(g, u):
                        s = u % 2
                        wait(dve, half_done, g - 1)
                        for k in range(TPG):
                            wait(dve, h_done, g * 2 * TPG + 2 * k + 2)
                            wait(dve, dot_done, g * TPG + k)
                            nc.vector.tensor_tensor_reduce(junk_v[:, :], hs[:, s, k, 0:D], hd[:, s, k, :], 1.0, 0.0,
                                                           ALU.mult, ALU.add,
                                                           accum_out=dot[:, s, k:k + 1]).then_inc(dot_done, 1)
                        wait(dve, sq_done, (g + 1) * 2 * TPG)
                        wait(dve, v_eps_done, 2 * g + 2)
                        nc.vector.scalar_tensor_tensor(rs_in[:, s, 0:2, :], var_eps[:, :, :], NORM_EPS * NORM_EPS,
                                                       sq[:, s, :, :], ALU.mult, ALU.max).then_inc(rs_in_done, 1)

                    def maxima(g, u):
                        s = u % 2
                        wait(dve, rs_done, g + 1)
                        wait(dve, dot_done, (g + 1) * TPG)
                        wait(dve, score_done, g)
                        nc.vector.scalar_tensor_tensor(half[:, :], dot[:, s, :], params[:, 6:7], rs[:, s, 0, :],
                                                       ALU.mult, ALU.mult).then_inc(half_done, 1)
                        wait(dve, half_done, g + 1)
                        wait(dve, erow_done, g - 1)
                        nc.vector.tensor_tensor(score[:, s, :], half[:, :], rs[:, s, 1, :],
                                                ALU.mult).then_inc(score_done, 1)
                        nc.vector.tensor_tensor(hs[:, s, :, D], rs_in[:, s, 2, :], rs[:, s, 2, :],
                                                ALU.mult).then_inc(aug_done, 1)
                        wait(dve, score_done, g + 1)
                        wait(dve, pw_done, g * TPG)
                        nc.vector.tensor_copy(ev[:, :, 0], score[:, s, :]).then_inc(ev_set, 1)
                        wait(dve, drow_done, g + 1)
                        wait(dve, max_done, g * TPG)
                        for k in range(TPG):
                            nc.vector.tensor_scalar(pen[:, k, :], D_ps[s][:, k * P:(k + 1) * P],
                                                    slot_f[:, u, 0, k:k + 1], LOWEST, ALU.not_equal,
                                                    ALU.mult).then_inc(pen_done, 1)
                        wait(dve, erow_done, g + 1)
                        wait(dve, ev_set, g + 1)
                        for k in range(TPG):
                            wait(dve, cm_done, g * TPG + k + 1)
                            nc.vector.tensor_scalar(ev[:, k, 1:2], M_ps[:, k:k + 1], slot_f[:, u, 1, k:k + 1], None,
                                                    ALU.add).then_inc(v_done, 1)
                            wait_apart(dve, (v_done, g * TPG + k + 1), (pen_done, g * TPG + k + 1),
                                       (ev_done, (g - 1) * TPG + k + 1), (cm_done, (g - 1) * TPG + k + 2))
                            nc.vector.tensor_tensor_reduce(pen[:, k, :], pen[:, k, :], E_ps[s][:, k * P:(k + 1) * P],
                                                           1.0, ev[:, k, 1:2], ALU.add, ALU.max,
                                                           accum_out=smax[:, k:k + 1]).then_inc(max_done, 1)
                            wait(dve, max_done, g * TPG + k + 1)
                            nc.vector.tensor_scalar(ev[:, k, :], ev[:, k, :], smax[:, k:k + 1], None,
                                                    ALU.subtract).then_inc(ev_done, 1)

                    def sums(g, u):
                        s = u % 2
                        wait(dve, pw_done, (g + 1) * TPG)
                        wait(dve, wsel_done, g * TPG)
                        nc.vector.tensor_tensor(p_rstd[:, :], pw[:, s, :, 0], rs[:, s, 2, :],
                                                ALU.mult).then_inc(p_rstd_done, 1)
                        wait(dve, p_rstd_done, g + 1)
                        for k in range(TPG):
                            wait(dve, u_done, (g - 1) * TPG + k + 1)
                            nc.vector.tensor_scalar(wsel[:, k, :], D_ps[s][:, k * P:(k + 1) * P],
                                                    slot_f[:, u, 0, k:k + 1], p_rstd[:, k:k + 1], ALU.is_equal,
                                                    ALU.mult).then_inc(wsel_done, 1)
                        wait(dve, scattered[(u - 2) % RING], laps(g - 2, (u - 2) % RING, 16 * TPG))
                        for k in range(TPG):
                            wait(dve, cu_done, g * TPG + k + 1)
                            wait(dve, part_done, g * TPG + k + 1)
                            wait(dve, row_done, g * TPG + k - 1)
                            nc.vector.scalar_tensor_tensor(acc[:, k % 2, :], C_ps[:, 0:AUG], pw[:, s, k, 1:2],
                                                           part[:, k % 2, :], ALU.mult, ALU.add).then_inc(acc_done, 1)
                            wait(dve, acc_done, g * TPG + k + 1)
                            nc.vector.reciprocal(rden[:, k:k + 1], acc[:, k % 2, D:AUG]).then_inc(rden_done, 1)
                            wait(dve, rden_done, g * TPG + k + 1)
                            nc.vector.scalar_tensor_tensor(rows[:, s, k, :], acc[:, k % 2, 0:D], rden[:, k:k + 1],
                                                           xd[:, u, k, :], ALU.mult, ALU.add).then_inc(row_done, 1)
                    pipeline(dve, (slots, 2), (moments, 1), (maxima, 0), (products, 1), (sums, 0))

                @block.tensor
                def _(pe):
                    pe.wait_ge(carry_set, 2)

                    def dst_rows(g, u):
                        s = u % 2
                        wait(pe, idx_ready, g + 1)
                        wait(pe, wsel_done, (g - 1) * TPG)
                        for k in range(TPG):
                            n = nc.tensor.matmul(D_ps[s][:, k * P:(k + 1) * P],
                                                 slot_f[:, u, 0, k:k + 1].broadcast_to([P, P]), ident[:, :],
                                                 start=True, stop=True)
                        n.then_inc(drow_done, 1)

                    def score_rows(g, u):
                        s = u % 2
                        wait(pe, score_done, g + 1)
                        wait(pe, max_done, (g - 1) * TPG)
                        for k in range(TPG):
                            n = nc.tensor.matmul(E_ps[s][:, k * P:(k + 1) * P],
                                                 score[:, s, k:k + 1].broadcast_to([P, P]), ident[:, :],
                                                 start=True, stop=True)
                        n.then_inc(erow_done, 1)
                        for k in range(TPG):
                            wait(pe, max_done, g * TPG + k)
                            wait(pe, v_done, (g - 1) * TPG + k + 1)
                            before = (k - 1) % TPG
                            nc.tensor.matmul(M_ps[:, k:k + 1], pick_last[:, :], smax[:, before:before + 1], start=True,
                                             stop=True).then_inc(cm_done, 1)

                    def segment_sums(g, u):
                        s = u % 2
                        wait(pe, aug_done, g + 1)
                        for k in range(TPG):
                            wait(pe, wsel_done, g * TPG + k + 1)
                            wait(pe, h_done, g * 2 * TPG + 2 * k + 1)
                            wait(pe, part_done, g * TPG + k - 1)
                            nc.tensor.matmul(U_ps[k % 2][:, 0:AUG], wsel[:, k, :], hs[:, s, k, :], start=True,
                                             stop=True).then_inc(u_done, 1)
                            wait(pe, acc_done, g * TPG + k)
                            nc.tensor.matmul(C_ps[:, 0:AUG], pick_last[:, :], acc[:, (k - 1) % 2, :], start=True,
                                             stop=True).then_inc(cu_done, 1)
                    pipeline(pe, (dst_rows, 0), (score_rows, 0), (segment_sums, 0))

        def mlp_front(tag, gather_rows, side, side_sorted, w_sb, bias_col, y_dram):
            with ExitStack() as c1:
                def sb1(name, shape, dt=fp32):
                    return c1.enter_context(nc.sbuf_tensor(tag + name, shape, dt))

                pass_sems = []

                def sem1(name):
                    pass_sems.append(nc.alloc_semaphore(name=tag + name))
                    return pass_sems[-1]
                xs = sb1("xs", [P, RING, TPG, D])
                sd = sb1("sd", [P, RING, TPG, D])
                hs = sb1("hs", [P, 2, TPG, D])
                hT = sb1("hT", [P, 2, GW])
                sT = sb1("sT", [P, 2, GW])
                yT = sb1("yT", [P, RING, GW])
                st6 = sb1("st6", [P, TPG, 6])
                mv = sb1("mv", [P, 2, TPG, 2])
                var_eps = sb1("var_eps", [P, 2, TPG])
                rstd = sb1("rstd", [P, 2, TPG])
                shift = sb1("shift", [P, 2, TPG])
                idx_ready = sem1("idx_ready")
                rows_in = [sem1(f"rows_in{u}") for u in range(RING)]
                side_in = [sem1(f"side_in{u}") for u in range(RING)]
                y_out = [sem1(f"y_out{u}") for u in range(RING)]
                st_done, mv_done, v_eps_done, rstd_done, shift_done = (
                    sem1(n) for n in ("st_done", "mv_done", "v_eps_done", "rstd_done", "shift_done"))
                h_done, hT_ps_done, sT_ps_done = sem1("h_done"), sem1("hT_ps_done"), sem1("sT_ps_done")
                hT_done, sT_done, y_ps_done, y_done, bn_done = (
                    sem1(n) for n in ("hT_done", "sT_done", "y_ps_done", "y_done", "bn_done"))
                row_dmas = TPG if gather_rows else 1

                with nc.Block() as block:
                    @block.sync
                    def _(sp):
                        if gather_rows:
                            unsorted_flag = sp.value_load(unsorted[0:1, 0:1], min_val=0, max_val=1)

                        def load_side(g, u):
                            wait_apart(sp, (sT_ps_done, g - RING + 1))
                            if gather_rows:
                                with sp.If(unsorted_flag > 0):
                                    for a, b in row_moves(side_sorted, sd[:, u, :, :], g, True):
                                        sp.dma_start(a, b).then_inc(side_in[u], 16)
                                with sp.Else():
                                    for a, b in row_moves(side, sd[:, u, :, :], g, True):
                                        sp.dma_start(a, b).then_inc(side_in[u], 16)
                                sp.end_ifs()
                                return
                            for a, b in row_moves(side, sd[:, u, :, :], g, True):
                                sp.dma_start(a, b).then_inc(side_in[u], 16)

                        def load_rows(g, u):
                            wait_apart(sp, (h_done, g - RING + 1))
                            for a, b in row_moves(x1, xs[:, u, :, :], g, True):
                                sp.dma_start(a, b).then_inc(rows_in[u], 16)

                        def store_y(g, u):
                            wait_apart(sp, (y_done, g + 1))
                            sp.dma_start(y_dram[:, bass.ds(g * GW, GW)], yT[:, u, :]).then_inc(y_out[u], 16)
                        if gather_rows:
                            pipeline(sp, (load_side, 2), (store_y, -1))
                        else:
                            pipeline(sp, (load_rows, 3), (load_side, 2), (store_y, -1))
                        for u in range(RING):
                            sp.wait_ge(y_out[u], 16 * len(range(u, G, RING)))

                    @block.gpsimd
                    def _(pool):
                        last_row = pool.to_reg(N - 1) if gather_rows else None

                        def gather(g, u):
                            wait_apart(pool, (idx_ready, g + 1), (h_done, g - RING + 1))
                            for k in range(TPG):
                                nc.gpsimd.indirect_dma_start(
                                    xs[:, u, k, :], None, x1,
                                    bass.IndirectOffsetOnAxis(ap=slot_i[:, u, 0, k:k + 1], axis=0),
                                    bounds_check=last_row, oob_is_err=False).then_inc(rows_in[u], 16)

                        def rsqrt(g, u):
                            wait(pool, v_eps_done, g + 1)
                            wait(pool, h_done, g - 1)
                            wait(pool, shift_done, g - 1)
                            nc.gpsimd.tensor_tensor(rstd[:, u % 2, :], var_eps[:, u % 2, :],
                                                    minus_half[:, 0:TPG], ALU.pow).then_inc(rstd_done, 1)
                        if gather_rows:
                            pipeline(pool, (gather, 3), (rsqrt, 2))
                        else:
                            pipeline(pool, (rsqrt, 2))

                    @block.scalar
                    def _(act):
                        def normalise(g, u):
                            wait(act, shift_done, g + 1)
                            wait(act, hT_ps_done, g - 1)
                            for k in range(TPG):
                                n = nc.scalar.activation(hs[:, u % 2, k, :], xs[:, u, k, :], ACT.Relu,
                                                         bias=shift[:, u % 2, k:k + 1],
                                                         scale=rstd[:, u % 2, k:k + 1])
                            n.then_inc(h_done, 1)

                        def copy_side(g, u):
                            wait(act, sT_ps_done, g + 1)
                            wait(act, y_ps_done, g - 1)
                            nc.scalar.copy(sT[:, u % 2, :], ps[2 + u % 2][:, :]).then_inc(sT_done, 1)

                        def add_bias(g, u):
                            wait(act, y_ps_done, g + 1)
                            wait(act, y_out[u], laps(g, u, 16) - 16)
                            wait(act, bn_done, g - RING + 1)
                            nc.scalar.activation(yT[:, u, :], ps[4 + u % 2][:, :], ACT.Identity,
                                                 bias=params[:, bias_col:bias_col + 1], scale=1.0).then_inc(y_done, 1)
                        pipeline(act, (normalise, 1), (copy_side, 1), (add_bias, 0))

                    @block.vector
                    def _(dve):
                        def slots(g, u):
                            wait(dve, rows_in[u], laps(g, u, 16 * TPG) - 16 * TPG)
                            load_slots(g, u, idx_ready)

                        def moments(g, u):
                            wait(dve, rows_in[u], laps(g, u, 16 * row_dmas)
                                 + (16 if is_tail(g) and not gather_rows else 0))
                            wait(dve, mv_done, g)
                            for k in range(TPG):
                                n = nc.vector.bn_stats(st6[:, k, :], xs[:, u, k, :])
                            n.then_inc(st_done, 1)
                            wait_apart(dve, (st_done, g + 1), (shift_done, g - 1))
                            for k in range(TPG):
                                n = nc.vector.bn_aggr(mv[:, u % 2, k, :], st6[:, k, :])
                            n.then_inc(mv_done, 1)
                            wait(dve, mv_done, g + 1)
                            wait(dve, rstd_done, g - 1)
                            nc.vector.tensor_scalar(var_eps[:, u % 2, :], mv[:, u % 2, :, 1], LN_EPS, None,
                                                    ALU.add).then_inc(v_eps_done, 1)

                        def shifts(g, u):
                            wait(dve, rstd_done, g + 1)
                            wait(dve, h_done, g - 1)
                            nc.vector.scalar_tensor_tensor(shift[:, u % 2, :], mv[:, u % 2, :, 0], -1.0,
                                                           rstd[:, u % 2, :], ALU.mult,
                                                           ALU.mult).then_inc(shift_done, 1)

                        def copy_h(g, u):
                            wait(dve, hT_ps_done, g + 1)
                            wait(dve, y_ps_done, g - 1)
                            nc.vector.tensor_copy(hT[:, u % 2, :], ps[u % 2][:, :]).then_inc(hT_done, 1)

                        def count_y(g, u):
                            wait(dve, y_done, g + 1)
                            n = TAIL if is_tail(g) else GW
                            nc.vector.bn_stats(bn_sum[:, bass.ds(g, 1), :].rearrange("p o c -> p (o c)"),
                                               yT[:, u, 0:n]).then_inc(bn_done, 1)
                        if gather_rows:
                            pipeline(dve, (slots, 3), (moments, 2), (shifts, 1), (copy_h, 0), (count_y, -1))
                        else:
                            pipeline(dve, (moments, 2), (shifts, 1), (copy_h, 0), (count_y, -1))

                    @block.tensor
                    def _(pe):
                        def turn_side(g, u):
                            wait(pe, side_in[u], laps(g, u, 16) + (16 if is_tail(g) else 0))
                            wait(pe, sT_done, g - 1)
                            for k in range(TPG):
                                n = nc.tensor.transpose(ps[2 + u % 2][:, k * P:(k + 1) * P], sd[:, u, k, :],
                                                        ident[:, :])
                            n.then_inc(sT_ps_done, 1)

                        def turn_h(g, u):
                            wait(pe, h_done, g + 1)
                            wait(pe, hT_done, g - 1)
                            for k in range(TPG):
                                n = nc.tensor.transpose(ps[u % 2][:, k * P:(k + 1) * P], hs[:, u % 2, k, :],
                                                        ident[:, :])
                            n.then_inc(hT_ps_done, 1)

                        def product(g, u):
                            wait(pe, hT_done, g + 1)
                            wait(pe, sT_done, g + 1)
                            wait(pe, y_done, g - 1)
                            nc.tensor.matmul(ps[4 + u % 2][:, :], w_sb[:, 0, :], hT[:, u % 2, :], start=True, stop=False)
                            nc.tensor.matmul(ps[4 + u % 2][:, :], w_sb[:, 1, :], sT[:, u % 2, :], start=False,
                                             stop=True).then_inc(y_ps_done, 1)
                        pipeline(pe, (turn_side, 1), (turn_h, 0), (product, 0))
                nc.clear_and_free_semaphores(pass_sems)
                nc.all_engine_barrier()

        def bn_coefficients(pool, dve, var_ready, inv_ready, step, gamma_col, beta_col):
            if dve is None:
                pool.wait_ge(var_ready, 1)
                nc.gpsimd.tensor_scalar(bn_rstd[:, :], bn_mv[:, 1:2], BN_EPS, None, ALU.add).then_inc(inv_ready, 1)
                pool.wait_ge(inv_ready, 1)
                nc.gpsimd.tensor_tensor(bn_rstd[:, :], bn_rstd[:, :], minus_half[:, 0:1], ALU.pow).then_inc(inv_ready, 1)
                return
            nc.vector.bn_aggr(bn_mv[:, :], bn_sum[:, :, :].rearrange("p g c -> p (g c)")).then_inc(var_ready, 1)
            dve.wait_ge(var_ready, 1)
            dve.wait_ge(inv_ready, 2)
            nc.vector.tensor_tensor(bn_s[:, :], bn_rstd[:, :], params[:, gamma_col:gamma_col + 1], ALU.mult).then_inc(step, 1)
            dve.wait_ge(step, 1)
            nc.vector.tensor_tensor(bn_tmp[:, :], bn_mv[:, 0:1], bn_s[:, :], ALU.mult).then_inc(step, 1)
            dve.wait_ge(step, 2)
            nc.vector.tensor_tensor(bn_t[:, :], params[:, beta_col:beta_col + 1], bn_tmp[:, :],
                                    ALU.subtract).then_inc(step, 1)

        mlp_front("p2_", True, edge_attr, ea_sorted, w1_sb, 0, y1)

        with ExitStack() as c1:
            def sb1(name, shape, dt=fp32):
                return c1.enter_context(nc.sbuf_tensor("p3_" + name, shape, dt))

            def sem1(name):
                return c1.enter_context(nc.semaphore("p3_" + name))
            yT = sb1("yT", [P, RING, GW])
            ex = sb1("ex", [P, 2, GW])
            rl = sb1("rl", [P, 2, GW])
            el = sb1("el", [P, 2, GW])
            h1 = sb1("h1", [P, 2, TPG, AUG])
            sel = sb1("sel", [P, 2, TPG, D])
            part = sb1("part", [P, 2, AUG])
            acc = sb1("acc", [P, 2, AUG])
            cnt = sb1("cnt", [P, TPG])
            rden = sb1("rden", [P, TPG])
            rows = sb1("rows", [P, 2, TPG, D])
            D_ps, T_ps, U_ps, C_ps = [ps[0], ps[1]], [ps[2], ps[3]], [ps[4], ps[5]], ps[6]
            init_set, bn_var, bn_inv, bn_step, idx_ready = (
                sem1(n) for n in ("init_set", "bn_var", "bn_inv", "bn_step", "idx_ready"))
            y_in = [sem1(f"y_in{u}") for u in range(RING)]
            scattered = [sem1(f"scattered{u}") for u in range(RING)]
            ex_done, rl_done, el_done, elT_done, h1_done = (
                sem1(n) for n in ("ex_done", "rl_done", "el_done", "elT_done", "h1_done"))
            drow_done, sel_done, u_done, part_done, cu_done = (
                sem1(n) for n in ("drow_done", "sel_done", "u_done", "part_done", "cu_done"))
            acc_done, cnt_done, rden_done, row_done = (
                sem1(n) for n in ("acc_done", "cnt_done", "rden_done", "row_done"))

            with nc.Block() as block:
                @block.sync
                def _(sp):
                    def load_y(g, u):
                        wait_apart(sp, (rl_done, g - RING + 1))
                        sp.dma_start(yT[:, u, :], y1[:, bass.ds(g * GW, GW)]).then_inc(y_in[u], 16)
                    pipeline(sp, (load_y, 3))

                @block.gpsimd
                def _(pool):
                    last_row = pool.to_reg(N - 1)
                    bn_coefficients(pool, None, bn_var, bn_inv, bn_step, 1, 2)

                    pool.wait_ge(agg_zero, 16 * len(zero_pieces))

                    def scatter(g, u):
                        for k in range(TPG):
                            wait_apart(pool, (row_done, g * TPG + k + 1))
                            nc.gpsimd.indirect_dma_start(
                                agg, bass.IndirectOffsetOnAxis(ap=slot_i[:, u, 2, k:k + 1], axis=0),
                                rows[:, u % 2, k, :], None, bounds_check=last_row,
                                oob_is_err=False).then_inc(scattered[u], 16)
                    pipeline(pool, (scatter, 0))
                    for u in range(RING):
                        pool.wait_ge(scattered[u], 16 * TPG * len(range(u, G, RING)))

                @block.scalar
                def _(act):
                    act.wait_ge(bn_step, 3)

                    def branches(g, u):
                        wait(act, y_in[u], laps(g, u, 16))
                        wait(act, el_done, g - 1)
                        nc.scalar.activation(ex[:, u % 2, :], yT[:, u, :], ACT.Exp, bias=bn_t[:, :],
                                             scale=bn_s[:, :]).then_inc(ex_done, 1)
                        nc.scalar.activation(rl[:, u % 2, :], yT[:, u, :], ACT.Relu, bias=bn_t[:, :],
                                             scale=bn_s[:, :]).then_inc(rl_done, 1)

                    def edge_major(g, u):
                        wait(act, elT_done, g + 1)
                        wait(act, u_done, (g - 1) * TPG)
                        if isinstance(g, int) and g < 2:
                            wait(act, init_set, 2)
                        nc.scalar.activation(h1[:, u % 2, :, 0:D],
                                             T_ps[u % 2][:, :].rearrange("p (k f) -> p k f", k=TPG),
                                             ACT.Copy, bias=-1.0).then_inc(h1_done, 1)

                    def parts(g, u):
                        for k in range(TPG):
                            wait(act, u_done, g * TPG + k + 1)
                            wait(act, acc_done, g * TPG + k - 1)
                            nc.scalar.copy(part[:, k % 2, :], U_ps[k % 2][:, 0:AUG]).then_inc(part_done, 1)
                    pipeline(act, (branches, 2), (edge_major, 1), (parts, 0))

                @block.vector
                def _(dve):
                    bn_coefficients(None, dve, bn_var, bn_inv, bn_step, 1, 2)
                    nc.vector.memset(h1[:, :, :, D:AUG], 1.0).then_inc(init_set, 1)
                    nc.vector.memset(acc[:, (TPG - 1) % 2, :], 0.0).then_inc(init_set, 1)

                    def slots(g, u):
                        load_slots(g, u, idx_ready, scattered)

                    def join(g, u):
                        wait(dve, ex_done, g + 1)
                        wait(dve, rl_done, g + 1)
                        wait(dve, elT_done, g - 1)
                        nc.vector.scalar_tensor_tensor(el[:, u % 2, :], ex[:, u % 2, :], 1.0, rl[:, u % 2, :], ALU.min,
                                                       ALU.add).then_inc(el_done, 1)

                    def selectors(g, u):
                        wait(dve, drow_done, g + 1)
                        wait(dve, idx_ready, g + 1)
                        wait(dve, u_done, (g - 1) * TPG)
                        for k in range(TPG):
                            nc.vector.tensor_scalar(sel[:, u % 2, k, :], D_ps[u % 2][:, k * P:(k + 1) * P],
                                                    slot_f[:, u, 0, k:k + 1], None,
                                                    ALU.is_equal).then_inc(sel_done, 1)

                    def means(g, u):
                        wait(dve, scattered[(u - 2) % RING], laps(g - 2, (u - 2) % RING, 16 * TPG))
                        for k in range(TPG):
                            wait(dve, cu_done, g * TPG + k + 1)
                            wait(dve, part_done, g * TPG + k + 1)
                            wait(dve, row_done, g * TPG + k - 1)
                            nc.vector.scalar_tensor_tensor(acc[:, k % 2, :], C_ps[:, 0:AUG], slot_f[:, u, 2, k:k + 1],
                                                           part[:, k % 2, :], ALU.mult, ALU.add).then_inc(acc_done, 1)
                            wait(dve, acc_done, g * TPG + k + 1)
                            nc.vector.tensor_scalar(cnt[:, k:k + 1], acc[:, k % 2, D:AUG], 1.0, None,
                                                    ALU.max).then_inc(cnt_done, 1)
                            wait(dve, cnt_done, g * TPG + k + 1)
                            nc.vector.reciprocal(rden[:, k:k + 1], cnt[:, k:k + 1]).then_inc(rden_done, 1)
                            wait(dve, rden_done, g * TPG + k + 1)
                            nc.vector.tensor_scalar(rows[:, u % 2, k, :], acc[:, k % 2, 0:D], rden[:, k:k + 1], None,
                                                    ALU.mult).then_inc(row_done, 1)
                    pipeline(dve, (slots, 2), (join, 2), (selectors, 1), (means, 0))

                @block.tensor
                def _(pe):
                    pe.wait_ge(init_set, 2)

                    def dst_rows(g, u):
                        wait(pe, idx_ready, g + 1)
                        wait(pe, sel_done, (g - 1) * TPG)
                        for k in range(TPG):
                            n = nc.tensor.matmul(D_ps[u % 2][:, k * P:(k + 1) * P],
                                                 slot_f[:, u, 0, k:k + 1].broadcast_to([P, P]), ident[:, :],
                                                 start=True, stop=True)
                        n.then_inc(drow_done, 1)

                    def turn_el(g, u):
                        wait(pe, el_done, g + 1)
                        wait(pe, h1_done, g - 1)
                        for k in range(TPG):
                            n = nc.tensor.transpose(T_ps[u % 2][:, k * P:(k + 1) * P],
                                                    el[:, u % 2, k * P:(k + 1) * P], ident[:, :])
                        n.then_inc(elT_done, 1)

                    def segment_sums(g, u):
                        wait(pe, h1_done, g + 1)
                        for k in range(TPG):
                            wait(pe, sel_done, g * TPG + k + 1)
                            wait(pe, part_done, g * TPG + k - 1)
                            nc.tensor.matmul(U_ps[k % 2][:, 0:AUG], sel[:, u % 2, k, :], h1[:, u % 2, k, :], start=True,
                                             stop=True).then_inc(u_done, 1)
                            wait(pe, acc_done, g * TPG + k)
                            nc.tensor.matmul(C_ps[:, 0:AUG], pick_last[:, :], acc[:, (k - 1) % 2, :], start=True,
                                             stop=True).then_inc(cu_done, 1)
                    pipeline(pe, (dst_rows, 1), (turn_el, 1), (segment_sums, 0))

        mlp_front("p4_", False, agg, None, w2_sb, 3, y2)

        with ExitStack() as c1:
            def sb1(name, shape, dt=fp32):
                return c1.enter_context(nc.sbuf_tensor("p5_" + name, shape, dt))

            def sem1(name):
                return c1.enter_context(nc.semaphore("p5_" + name))
            yT = sb1("yT", [P, RING, GW])
            xr = sb1("xr", [P, RING, TPG, D])
            ex = sb1("ex", [P, 2, GW])
            rl = sb1("rl", [P, 2, GW])
            el = sb1("el", [P, 2, GW])
            res = sb1("res", [P, RING, TPG, D])
            bn_var, bn_inv, bn_step = sem1("bn_var"), sem1("bn_inv"), sem1("bn_step")
            y_in = [sem1(f"y_in{u}") for u in range(RING)]
            x_in = [sem1(f"x_in{u}") for u in range(RING)]
            stored = [sem1(f"stored{u}") for u in range(RING)]
            ex_done, rl_done, el_done, elT_done, res_done = (
                sem1(n) for n in ("ex_done", "rl_done", "el_done", "elT_done", "res_done"))

            with nc.Block() as block:
                @block.sync
                def _(sp):
                    def load(g, u):
                        wait_apart(sp, (rl_done, g - RING + 1))
                        sp.dma_start(yT[:, u, :], y2[:, bass.ds(g * GW, GW)]).then_inc(y_in[u], 16)
                        wait_apart(sp, (res_done, g - RING + 1))
                        for a, b in row_moves(x1, xr[:, u, :, :], g, True):
                            sp.dma_start(a, b).then_inc(x_in[u], 16)

                    def store(g, u):
                        wait_apart(sp, (res_done, g + 1))
                        for a, b in row_moves(out, res[:, u, :, :], g, False):
                            sp.dma_start(a, b).then_inc(stored[u], 16)
                    pipeline(sp, (load, 2), (store, -1))
                    for u in range(RING):
                        sp.wait_ge(stored[u], 16 * (len(range(u, G, RING)) + (1 if u == (G - 1) % RING else 0)))

                @block.gpsimd
                def _(pool):
                    bn_coefficients(pool, None, bn_var, bn_inv, bn_step, 4, 5)

                @block.scalar
                def _(act):
                    act.wait_ge(bn_step, 3)

                    def branches(g, u):
                        wait(act, y_in[u], laps(g, u, 16))
                        wait(act, el_done, g - 1)
                        nc.scalar.activation(ex[:, u % 2, :], yT[:, u, :], ACT.Exp, bias=bn_t[:, :],
                                             scale=bn_s[:, :]).then_inc(ex_done, 1)
                        nc.scalar.activation(rl[:, u % 2, :], yT[:, u, :], ACT.Relu, bias=bn_t[:, :],
                                             scale=bn_s[:, :]).then_inc(rl_done, 1)
                    pipeline(act, (branches, 1))

                @block.vector
                def _(dve):
                    bn_coefficients(None, dve, bn_var, bn_inv, bn_step, 4, 5)

                    def join(g, u):
                        wait(dve, ex_done, g + 1)
                        wait(dve, rl_done, g + 1)
                        wait(dve, elT_done, g - 1)
                        nc.vector.scalar_tensor_tensor(el[:, u % 2, :], ex[:, u % 2, :], 1.0, rl[:, u % 2, :], ALU.min,
                                                       ALU.add).then_inc(el_done, 1)

                    def residual(g, u):
                        wait(dve, elT_done, g + 1)
                        wait(dve, x_in[u], laps(g, u, 16) + (16 if is_tail(g) else 0))
                        wait(dve, stored[u], laps(g, u, 16) - 16)
                        nc.vector.scalar_tensor_tensor(res[:, u, :, :].rearrange("p k f -> p (k f)"), ps[u % 2][:, :],
                                                       -1.0, xr[:, u, :, :].rearrange("p k f -> p (k f)"), ALU.add,
                                                       ALU.add).then_inc(res_done, 1)
                    pipeline(dve, (join, 1), (residual, 0))

                @block.tensor
                def _(pe):
                    def turn_el(g, u):
                        wait(pe, el_done, g + 1)
                        wait(pe, res_done, g - 1)
                        for k in range(TPG):
                            n = nc.tensor.transpose(ps[u % 2][:, k * P:(k + 1) * P], el[:, u % 2, k * P:(k + 1) * P],
                                                    ident[:, :])
                        n.then_inc(elT_done, 1)
                    pipeline(pe, (turn_el, 1))


_INS = ["x", "src", "dst", "edge_attr_128", "L0_gnn_beta", "L1_gnn_W1", "L1_gnn_b1", "L1_gnn_g1", "L1_gnn_be1",
        "L1_gnn_W2", "L1_gnn_b2", "L1_gnn_g2", "L1_gnn_be2"]


def kernel(**inputs):
    import numpy as np
    import concourse.bacc as bacc
    from concourse.bass_utils import run_bass_kernel_spmd

    nc = bacc.Bacc("TRN2", target_bir_lowering=False, num_devices=1)
    arrays, args = {}, []
    for name in _INS:
        a = np.ascontiguousarray(inputs[name])
        arrays[f"in_{name}"] = a
        args.append(nc.dram_tensor(f"in_{name}", a.shape, mybir.dt.from_np(a.dtype), kind="ExternalInput").ap())
    shape = inputs["x"].shape
    args.append(nc.dram_tensor("out_x", shape, mybir.dt.float32, kind="ExternalOutput").ap())
    build_gnn(nc, *args)
    r = run_bass_kernel_spmd(nc, [arrays], core_ids=[0])
    return r.results[0]["out_x"]
```

```python
from contextlib import ExitStack

import concourse.bass as bass
from concourse import mybir

P = 128
TPG = 4
RING = 4
KEPT = 3
X1_PIECES = 32
X1_FIRST_PIECES = 4
ZERO_ROWS = 8
EARLY = 8
GW = P * TPG
FAR = float(2 ** 20)
LOWEST = -3.0e38
LN_EPS = 1e-5
BN_EPS = 1e-4
NORM_EPS = 1e-12
RSQRT_SEED = float(0x5F3759DF)
RSQRT_STEPS = 10


def build_gnn(nc, x, src, dst, edge_attr, beta, W1, b1, g1, be1, W2, b2, g2, be2, out):
    fp32, i32 = mybir.dt.float32, mybir.dt.int32
    ALU, ACT = mybir.AluOpType, mybir.ActivationFunctionType
    N, D = x.shape
    E = src.shape[0]
    assert D == P and E == N
    G = -(-N // GW)
    assert G >= 4 * RING
    T = G * TPG
    TAIL = N - (G - 1) * GW
    TAIL_FULL, TAIL_REST = TAIL // P, TAIL % P
    TB = -(-T // P)
    AUG = D + 1

    ctx = ExitStack()
    with ctx:
        def sb(name, shape, dt=fp32):
            return ctx.enter_context(nc.sbuf_tensor(name, shape, dt))

        def sem(name):
            return ctx.enter_context(nc.semaphore(name))

        def dram(name, shape):
            return nc.dram_tensor(name, shape, fp32, kind="Internal").ap()

        x1 = dram("x1", [N, D])
        agg = dram("agg", [N, D])
        ea_sorted = dram("ea_sorted", [T * P, D])
        src_sorted = nc.dram_tensor("src_sorted", [T * P, 1], i32, kind="Internal").ap()
        dst_sorted = nc.dram_tensor("dst_sorted", [T * P, 1], i32, kind="Internal").ap()
        y_spilled = dram("y_spilled", [P, G * GW])

        wait_carrier = sem("wait_carrier")
        ps = [ctx.enter_context(nc.psum_tensor(f"bank{i}", [P, GW], fp32)) for i in range(8)]

        ident = sb("ident", [P, P])
        pick_last = sb("pick_last", [P, P])
        shift_up = sb("shift_up", [P, P])
        wrap_up = sb("wrap_up", [P, P])
        minus_half = sb("minus_half", [P, TPG])
        earlier = sb("earlier", [P, P])
        ones_col = sb("ones_col", [P, 1])
        zeros = sb("zeros", [P, ZERO_ROWS * D])
        unsorted = sb("unsorted", [1, 1], i32)
        x1_init, agg_zero = [[sem(f"{name}{i}") for i in range(2)] for name in ("x1_init", "agg_zero")]
        edge_f = sb("edge_f", [P, G, 4, TPG])
        edge_i = sb("edge_i", [P, G, 3, TPG], i32)
        slot_f = sb("slot_f", [P, RING, 4, TPG])
        slot_g = sb("slot_g", [P, RING, 2, TPG], i32)
        slot_s = sb("slot_s", [P, RING, TPG], i32)
        w1_sb = sb("w1_sb", [P, 2, D])
        w2_sb = sb("w2_sb", [P, 2, D])
        params = sb("params", [P, 7])
        bn_sum = sb("bn_sum", [P, G, 6])
        bn_mv = sb("bn_mv", [P, 2])
        bn_s = sb("bn_s", [P, 1])
        bn_t = sb("bn_t", [P, 1])
        bn_tmp = sb("bn_tmp", [P, 1])
        bn_rstd = sb("bn_rstd", [P, 1])

        def pipeline(*parts, peel=0):
            eng, parts = parts[0], parts[1:]

            def step(g, u):
                for part, ahead in parts:
                    j = g + ahead
                    if not isinstance(j, int) or 0 <= j < G:
                        part(j, (u + ahead) % RING)
            most, least = max(a for _, a in parts), min(a for _, a in parts)
            first = -(-max(RING - 1 - least, peel) // RING) * RING
            stop = first + (G - 1 - most - first) // RING * RING
            for g in range(-most, first):
                step(g, g % RING)
            with eng.Fori(first // RING, stop // RING) as turn:
                for u in range(RING):
                    step(turn * RING + u, u)
            for g in range(stop, G - least):
                step(g, g % RING)

        def wait(eng, s, value):
            if not isinstance(value, int) or value > 0:
                eng.wait_ge(s, value)

        def wait_apart(eng, *waits):
            for s, v in waits:
                wait(eng, s, v)
            if any(not isinstance(v, int) for _, v in waits):
                eng.sem_inc(wait_carrier, 1)

        def is_tail(g):
            return isinstance(g, int) and g == G - 1

        def laps(g, u, per):
            return (g - u) * (per // RING) + per

        def gather_slots(j, u, ready):
            nc.vector.tensor_copy(slot_g[:, u, :, :],
                                  edge_i[:, bass.ds(j, 1), 0:2, :].rearrange("p o a k -> p (o a) k")).then_inc(ready, 1)

        def scatter_slots(j, u, scattered):
            if scattered is not None:
                wait(nc.vector, scattered[u], laps(j, u, 16 * TPG) - 16 * TPG)
            nc.vector.tensor_copy(slot_s[:, u, :], edge_i[:, bass.ds(j, 1), 2, :].rearrange("p o k -> p (o k)"))

        def segment_slots(j, u, ready):
            nc.vector.tensor_copy(slot_f[:, u, :, :],
                                  edge_f[:, bass.ds(j, 1), :, :].rearrange("p o a k -> p (o a) k")).then_inc(ready, 1)

        def row_moves(dram_rows, tile, g, load):
            if is_tail(g):
                r0 = g * GW
                full = dram_rows[r0:r0 + TAIL_FULL * P, :].rearrange("(k p) f -> p k f", p=P)
                rest = dram_rows[r0 + TAIL_FULL * P:N, :]
                pieces = [(full, tile[:, 0:TAIL_FULL, :]), (rest, tile[0:TAIL_REST, TAIL_FULL, :])]
            else:
                pieces = [(dram_rows[bass.ds(g * GW, GW), :].rearrange("(k p) f -> p k f", p=P), tile)]
            return [(b, a) if load else (a, b) for a, b in pieces]

        def rsqrt_step(dve, i, y, x, t, before, done):
            wait(dve, done, before + i)
            if i == 0:
                n = nc.vector.tensor_scalar(y.bitcast(i32), x.bitcast(i32), -0.5, RSQRT_SEED, ALU.mult, ALU.add)
            elif i % 3 == 1:
                n = nc.vector.tensor_tensor(t, y, y, ALU.mult)
            elif i % 3 == 2:
                n = nc.vector.scalar_tensor_tensor(t, t, -0.5, x, ALU.mult, ALU.mult)
            else:
                n = nc.vector.scalar_tensor_tensor(y, t, 1.5, y, ALU.add, ALU.mult)
            n.then_inc(done, 1)

        def load_columns(sp, pieces, done):
            for to, frm in pieces:
                sp.dma_start(to, frm).then_inc(done, 16)

        def index_pieces(raw_i, lists, count):
            pieces = []
            for j, idx in enumerate(lists):
                for b in range(TB):
                    r0, r1 = b * P, min((b + 1) * P, count // P)
                    if r1 > r0:
                        pieces.append((raw_i[0:r1 - r0, j, b, :], idx[r0 * P:r1 * P].rearrange("(r c) -> r c", c=P)))
                r = count // P
                if count % P:
                    pieces.append((raw_i[r % P:r % P + 1, j, r // P, 0:count % P],
                                   idx[r * P:count].rearrange("(r c) -> r c", r=1)))
            return pieces

        with ExitStack() as c1:
            def sb1(name, shape, dt=fp32):
                return c1.enter_context(nc.sbuf_tensor(name, shape, dt))

            def sem1(name):
                return c1.enter_context(nc.semaphore(name))
            raw_i = sb1("raw_i", [P, 2, TB, P], i32)
            raw_f = sb1("raw_f", [P, 2, TB, P])
            src_f = sb1("src_f", [P, TB * P])
            dst_f = sb1("dst_f", [P, TB * P])
            falls = sb1("falls", [P, TB * P])
            fall = sb1("fall", [P, 1])
            unsorted_here = sb1("unsorted_here", [1, 1])

            raw_set, raw_in = sem1("raw_set"), sem1("raw_in")
            const_set, const_ready = sem1("const_set"), sem1("const_ready")
            small_in, zeros_set = sem1("small_in"), sem1("zeros_set")
            as_float, turned, placed = sem1("as_float"), sem1("turned"), sem1("placed")
            neigh, flag_step, fall_sum = sem1("neigh"), sem1("flag_step"), sem1("fall_sum")

            def next_destinations(pe):
                nc.tensor.matmul(ps[3][:, 0:T], shift_up[:, :], dst_f[:, 0:T], start=True, stop=False)
                return nc.tensor.matmul(ps[3][:, 0:T], wrap_up[:, :], dst_f[:, 1:T + 1], start=False, stop=True)

            def turn_lists(pe):
                for j in range(2):
                    for b in range(TB):
                        t = nc.tensor.transpose(ps[j][:, b * P:(b + 1) * P], raw_f[:, j, b, :], ident[:, :])
                return t

            first_pieces = index_pieces(raw_i, (src, dst), E)
            x1_cuts = [N * i // X1_PIECES for i in range(X1_PIECES + 1)]
            x1_pieces = list(zip(x1_cuts[:-1], x1_cuts[1:]))
            with nc.Block() as block:
                @block.sync
                def _(sp):
                    sp.wait_ge(raw_set, 2)
                    load_columns(sp, first_pieces, raw_in)
                    for j, v in enumerate((b1, g1, be1, b2, g2, be2)):
                        sp.dma_start(params[:, j:j + 1], v.rearrange("(p o) -> p o", o=1)).then_inc(small_in, 16)
                    sp.dma_start(params[:, 6:7],
                                 beta.rearrange("(p o) -> p o", p=1).broadcast_to([P, 1])).then_inc(small_in, 16)
                    sp.dma_start(w1_sb[:, :, :], W1.rearrange("(h k) c -> k h c", h=2)).then_inc(small_in, 16)
                    sp.dma_start(w2_sb[:, :, :], W2.rearrange("(h k) c -> k h c", h=2)).then_inc(small_in, 16)
                    for i, (a, b) in enumerate(x1_pieces[0:X1_FIRST_PIECES]):
                        sp.dma_start(x1[a:b, :], x[a:b, :]).then_inc(x1_init[i % 2], 16)
                    sp.wait_ge(small_in, 9 * 16)

                @block.gpsimd
                def _(pool):
                    nc.gpsimd.memset(raw_i[:, 0, :, :], 0).then_inc(raw_set, 1)
                    nc.gpsimd.memset(raw_i[:, 1, :, :], int(FAR)).then_inc(raw_set, 1)
                    nc.gpsimd.memset(minus_half[:, :], -0.5)
                    for m in (ident, pick_last, shift_up, wrap_up):
                        nc.gpsimd.memset(m[:, :], 0.0).then_inc(const_set, 1)
                    nc.gpsimd.memset(earlier[:, :], 1.0).then_inc(const_set, 1)
                    pool.wait_ge(const_set, 5)
                    for m, base in ((ident, 0), (shift_up, -1)):
                        nc.gpsimd.affine_select(out=m[:, :], in_=m[:, :], compare_op=ALU.not_equal, fill=1.0,
                                                base=base, pattern=[[-1, P]],
                                                channel_multiplier=1).then_inc(const_ready, 1)
                    nc.gpsimd.affine_select(out=pick_last[:, :], in_=pick_last[:, :], compare_op=ALU.not_equal,
                                            fill=1.0, base=-(P - 1), pattern=[[0, P]],
                                            channel_multiplier=1).then_inc(const_ready, 1)
                    nc.gpsimd.affine_select(out=wrap_up[:, P - 1:P], in_=wrap_up[:, P - 1:P],
                                            compare_op=ALU.not_equal, fill=1.0, base=0, pattern=[[0, 1]],
                                            channel_multiplier=1).then_inc(const_ready, 1)
                    nc.gpsimd.affine_select(out=earlier[:, :], in_=earlier[:, :], compare_op=ALU.is_gt, fill=0.0,
                                            base=0, pattern=[[-1, P]],
                                            channel_multiplier=1).then_inc(const_ready, 1)

                @block.vector
                def _(dve):
                    nc.vector.memset(zeros[:, :], 0.0)
                    nc.vector.memset(ones_col[:, :], 1.0).then_inc(zeros_set, 1)
                    dve.wait_ge(raw_in, 16 * len(first_pieces))
                    nc.vector.tensor_copy(raw_f[:, :, :, :], raw_i[:, :, :, :]).then_inc(as_float, 1)
                    dve.wait_ge(turned, 1)
                    nc.vector.tensor_copy(src_f[:, :], ps[0][:, 0:TB * P]).then_inc(placed, 1)
                    nc.vector.tensor_copy(dst_f[:, :], ps[1][:, 0:TB * P]).then_inc(placed, 1)
                    dve.wait_ge(neigh, 1)
                    nc.vector.tensor_tensor(falls[:, 0:T], dst_f[:, 0:T], ps[3][:, 0:T], ALU.is_gt).then_inc(flag_step, 1)
                    dve.wait_ge(flag_step, 1)
                    nc.vector.reduce_max(fall[:, :], falls[:, 0:T], mybir.AxisListType.X).then_inc(flag_step, 1)
                    dve.wait_ge(fall_sum, 1)
                    nc.vector.tensor_scalar(unsorted_here[:, :], ps[4][0:1, 0:1], 1.0, None, ALU.min).then_inc(flag_step, 1)
                    dve.wait_ge(flag_step, 3)
                    nc.vector.tensor_copy(unsorted[:, :], unsorted_here[:, :])

                @block.tensor
                def _(pe):
                    pe.wait_ge(const_ready, 5)
                    pe.wait_ge(as_float, 1)
                    turn_lists(pe).then_inc(turned, 1)
                    pe.wait_ge(placed, 2)
                    next_destinations(pe).then_inc(neigh, 1)
                    pe.wait_ge(flag_step, 2)
                    pe.wait_ge(zeros_set, 1)
                    nc.tensor.matmul(ps[4][0:1, 0:1], fall[:, :], ones_col[:, :], start=True,
                                     stop=True).then_inc(fall_sum, 1)

            with ExitStack() as c2:
                def sb2(name, shape, dt=fp32):
                    return c2.enter_context(nc.sbuf_tensor(name, shape, dt))

                def sem2(name):
                    return sem("sort_" + name)
                all_dst = sb2("all_dst", [P, T * P], mybir.dt.uint16)
                counted = sb2("counted", [P, T * P], mybir.dt.uint8)
                tied = sb2("tied", [P, P])
                col = sb2("col", [P, 1])
                limit = sb2("limit", [P, 1])
                below = sb2("below", [P, 1])
                ties = sb2("ties", [P, 1])
                rank = sb2("rank", [P, 1], i32)
                src_i = sb2("src_i", [P, 1], i32)
                dst_i = sb2("dst_i", [P, 1], i32)
                ea_row = sb2("ea_row", [P, D])
                col_set, col_row, row_set = sem2("col_set"), sem2("col_row"), sem2("row_set")
                limit_set, below_set, ties_set, rank_set, lowered = (
                    sem2(n) for n in ("limit_set", "below_set", "ties_set", "rank_set", "lowered"))
                ea_in, list_out, ea_out = sem2("ea_in"), sem2("list_out"), sem2("ea_out")
                reloaded, sorted_float, sorted_turned = sem2("reloaded"), sem2("float"), sem2("turned")
                again = index_pieces(raw_i, (src_sorted.rearrange("r o -> (r o)"),
                                             dst_sorted.rearrange("r o -> (r o)")), T * P)
                FULL = E // P

                def over_tiles(eng, tile, whole):
                    tile(0)
                    with eng.Fori(1, whole) as t:
                        tile(t)
                    for t in range(whole, T):
                        tile(t)

                def when_unsorted(eng, body):
                    flag = eng.value_load(unsorted[0:1, 0:1], min_val=0, max_val=1)
                    with eng.If(flag > 0):
                        body()
                    eng.end_ifs()

                with nc.Block() as block:
                    @block.sync
                    def _(sp):
                        def tile(t):
                            wait_apart(sp, (ea_out, t * 16))
                            rows = E - t * P if isinstance(t, int) and t >= FULL else P
                            if rows > 0:
                                sp.dma_start(ea_row[0:rows, :], edge_attr[bass.ds(t * P, rows), :]).then_inc(ea_in, 16)
                            else:
                                sp.sem_inc(ea_in, 16)

                        def body():
                            over_tiles(sp, tile, FULL)
                            sp.wait_ge(list_out, 2 * 16 * T)
                            load_columns(sp, again, reloaded)
                        when_unsorted(sp, body)

                    @block.gpsimd
                    def _(pool):
                        def tile(t):
                            for frm, to in ((src_i, src_sorted), (dst_i, dst_sorted), (ea_row, ea_sorted)):
                                if frm is src_i:
                                    wait_apart(pool, (rank_set, t + 1))
                                if frm is ea_row:
                                    wait_apart(pool, (ea_in, t * 16 + 16))
                                nc.gpsimd.indirect_dma_start(
                                    to, bass.IndirectOffsetOnAxis(ap=rank[:, 0:1], axis=0), frm[:, :], None,
                                    bounds_check=T * P - 1, oob_is_err=False
                                ).then_inc(ea_out if frm is ea_row else list_out, 16)

                        def body():
                            over_tiles(pool, tile, FULL)
                            pool.wait_ge(ea_out, 16 * T)
                        when_unsorted(pool, body)

                    @block.vector
                    def _(dve):
                        def spread(t):
                            wait(dve, col_row, t)
                            nc.vector.tensor_copy(col[:, :], dst_f[:, bass.ds(t, 1)]).then_inc(col_set, 1)
                            wait(dve, col_row, t + 1)
                            nc.vector.tensor_scalar(all_dst[:, bass.ds(t * P, P)], ps[0][:, 0:P], 1.0, 65535.0,
                                                    ALU.add, ALU.min).then_inc(row_set, 1)

                        def rank_tile(t):
                            own = all_dst[:, bass.ds(t * P, P)]
                            nc.vector.tensor_scalar(limit[:, :], dst_f[:, bass.ds(t, 1)], 1.0, 65535.0, ALU.add,
                                                    ALU.min).then_inc(limit_set, 1)
                            wait(dve, limit_set, t + 1)
                            wait(dve, lowered, t)
                            nc.vector.tensor_scalar(counted[:, :], all_dst[:, :], limit[:, :], 0.0, ALU.is_lt, ALU.add,
                                                    accum_out=below[:, :]).then_inc(below_set, 1)
                            nc.vector.scalar_tensor_tensor(tied[:, :], own, limit[:, :], earlier[:, :], ALU.is_equal,
                                                           ALU.mult, accum_out=ties[:, :]).then_inc(ties_set, 1)
                            wait(dve, below_set, t + 1)
                            wait(dve, ties_set, t + 1)
                            wait(dve, list_out, t * 32)
                            wait(dve, ea_out, t * 16)
                            nc.vector.tensor_copy(src_i[:, :], src_f[:, bass.ds(t, 1)])
                            nc.vector.tensor_copy(dst_i[:, :], dst_f[:, bass.ds(t, 1)])
                            nc.vector.tensor_tensor(rank[:, :], below[:, :], ties[:, :], ALU.add).then_inc(rank_set, 1)
                            nc.vector.tensor_scalar(own, own, 1.0, None, ALU.subtract).then_inc(lowered, 1)
                            wait(dve, lowered, t + 1)

                        def body():
                            over_tiles(dve, spread, T)
                            dve.wait_ge(row_set, T)
                            over_tiles(dve, rank_tile, T)
                            dve.wait_ge(reloaded, 16 * len(again))
                            nc.vector.tensor_copy(raw_f[:, :, :, :], raw_i[:, :, :, :]).then_inc(sorted_float, 1)
                            dve.wait_ge(sorted_turned, 1)
                            nc.vector.tensor_copy(src_f[:, :], ps[0][:, 0:TB * P])
                            nc.vector.tensor_copy(dst_f[:, :], ps[1][:, 0:TB * P])
                        when_unsorted(dve, body)

                    @block.tensor
                    def _(pe):
                        def spread(t):
                            wait(pe, col_set, t + 1)
                            wait(pe, row_set, t)
                            nc.tensor.matmul(ps[0][:, 0:P], col[:, 0:1].broadcast_to([P, P]), ident[:, :], start=True,
                                             stop=True).then_inc(col_row, 1)

                        def body():
                            over_tiles(pe, spread, T)
                            pe.wait_ge(sorted_float, 1)
                            pe.wait_ge(row_set, T)
                            turn_lists(pe).then_inc(sorted_turned, 1)
                        when_unsorted(pe, body)

            same = sb1("same", [P, TB * P])
            last = sb1("last", [P, TB * P])
            far = sb1("far", [P, TB * P])
            table_neigh, table_step, reach = sem1("table_neigh"), sem1("table_step"), sem1("reach")
            with nc.Block() as block:
                @block.vector
                def _(dve):
                    dst_g = dst_f[:, 0:T].rearrange("p (g k) -> p g k", k=TPG)
                    nc.vector.tensor_copy(edge_i[:, :, 0, :], src_f[:, 0:T].rearrange("p (g k) -> p g k", k=TPG))
                    nc.vector.tensor_copy(edge_f[:, :, 0, :], dst_g)
                    nc.vector.tensor_scalar(edge_i[:, :, 1, :], dst_g, float(N - 1), None, ALU.min)
                    dve.wait_ge(table_neigh, 1)
                    nc.vector.memset(same[:, 0:1], 0.0)
                    nc.vector.tensor_tensor(same[:, 1:T], dst_f[:, 1:T], ps[2][:, 0:T - 1],
                                            ALU.is_equal).then_inc(table_step, 1)
                    nc.vector.tensor_tensor(last[:, 0:T], dst_f[:, 0:T], ps[3][:, 0:T],
                                            ALU.is_equal).then_inc(table_step, 1)
                    dve.wait_ge(table_step, 2)
                    same_g = same[:, 0:T].rearrange("p (g k) -> p g k", k=TPG)
                    nc.vector.tensor_copy(edge_f[:, :, 2, :], same_g)
                    nc.vector.tensor_scalar(edge_f[:, :, 1, :], same_g, 1.0, -LOWEST, ALU.subtract, ALU.mult)
                    nc.vector.scalar_tensor_tensor(far[:, 0:T], last[:, 0:T], FAR, dst_f[:, 0:T],
                                                   ALU.mult, ALU.add).then_inc(table_step, 1)
                    dve.wait_ge(table_step, 3)
                    nc.vector.tensor_copy(edge_i[:, :, 2, :], far[:, 0:T].rearrange("p (g k) -> p g k", k=TPG))
                    dve.wait_ge(reach, 1)
                    nc.vector.tensor_scalar(edge_f[:, :, 3, :], ps[4][:, 0:T].rearrange("p (g k) -> p g k", k=TPG),
                                            1.0, -LOWEST, ALU.subtract, ALU.mult)

                @block.tensor
                def _(pe):
                    nc.tensor.matmul(ps[2][:, 0:T], pick_last[:, :], dst_f[:, 0:T], start=True, stop=True)
                    next_destinations(pe).then_inc(table_neigh, 1)
                    pe.wait_ge(table_step, 2)
                    nc.tensor.matmul(ps[4][:, 0:T], pick_last[:, :], same[:, 0:T], start=True,
                                     stop=True).then_inc(reach, 1)

        zero_pieces = []
        for a in range(0, N, ZERO_ROWS * P):
            rest = min(N - a, ZERO_ROWS * P)
            q = max(n for n in range(1, P + 1) if rest % n == 0 and rest // n <= ZERO_ROWS)
            zero_pieces.append((agg[a:a + rest, :].rearrange("(p r) f -> p (r f)", p=q), q, rest // q * D))

        with ExitStack() as c1:
            def sb1(name, shape, dt=fp32):
                return c1.enter_context(nc.sbuf_tensor("p1_" + name, shape, dt))

            def sem1(name):
                return c1.enter_context(nc.semaphore("p1_" + name))
            xs = sb1("xs", [P, RING, TPG, D])
            xd = sb1("xd", [P, RING, TPG, D])
            hs = sb1("hs", [P, RING, TPG, AUG])
            hd = sb1("hd", [P, 2, TPG, D])
            junk_a = sb1("junk_a", [P, 2, D])
            junk_v = sb1("junk_v", [P, D])
            st6 = sb1("st6", [P, 2, TPG, 6])
            mv = sb1("mv", [P, 2, TPG, 2])
            neg_mean = sb1("neg_mean", [P, 2, 2, TPG])
            var_eps = sb1("var_eps", [P, 2, 2, TPG])
            sq = sb1("sq", [P, 2, 2, TPG])
            dot = sb1("dot", [P, 2, TPG])
            rs_in = sb1("rs_in", [P, RING, 3, TPG])
            rs = sb1("rs", [P, 2, 3, TPG])
            root_tmp = sb1("root_tmp", [P, 3, TPG])
            half = sb1("half", [P, TPG])
            score = sb1("score", [P, 2, TPG])
            pen = sb1("pen", [P, TPG, D])
            tile_max = sb1("tile_max", [P, TPG])
            carry = sb1("carry", [P, 1 + TPG])
            carried = sb1("carried", [P, TPG])
            smax = sb1("smax", [P, TPG])
            ev = sb1("ev", [P, 2, TPG])
            pw = sb1("pw", [P, 2, 2, TPG])
            p_rstd = sb1("p_rstd", [P, TPG])
            wsel = sb1("wsel", [P, TPG, D])
            part = sb1("part", [P, 2, AUG])
            acc = sb1("acc", [P, TPG, AUG])
            rden = sb1("rden", [P, TPG])
            rows = sb1("rows", [P, RING, TPG, D])
            early_rows = sb1("early_rows", [P, EARLY, TPG, D])
            early_index = sb1("early_index", [P, EARLY, TPG], i32)
            D_ps, E_ps, U_ps = [ps[0], ps[1]], [ps[2], ps[3]], [ps[4], ps[5]]
            C_ps, M_ps = ps[6], ps[7]

            carry_set, gidx_ready, seg_ready = sem1("carry_set"), sem1("gidx_ready"), sem1("seg_ready")
            gathered = [sem1(f"gathered{u}") for u in range(RING)]
            scattered = [sem1(f"scattered{u}") for u in range(RING)]
            st_done, mv_done, mean_done, v_eps_done = (sem1(n) for n in ("st_done", "mv_done", "mean_done", "v_eps_done"))
            h_done, sq_done, dot_done = sem1("h_done"), sem1("sq_done"), sem1("dot_done")
            rs_in_done, rs_done, half_done, score_done = (sem1(n) for n in ("rs_in_done", "rs_done", "half_done", "score_done"))
            aug_done, drow_done, erow_done, pen_done = (sem1(n) for n in ("aug_done", "drow_done", "erow_done", "pen_done"))
            tmax_done, last_row_done, carry_done, carry_kept = (
                sem1(n) for n in ("tmax_done", "last_row_done", "carry_done", "carry_kept"))
            carried_done, max_done, ev_done = sem1("carried_done"), sem1("max_done"), sem1("ev_done")
            pw_done, p_rstd_done, wsel_done = sem1("pw_done"), sem1("p_rstd_done"), sem1("wsel_done")
            u_done, part_done, cu_done, acc_done = sem1("u_done"), sem1("part_done"), sem1("cu_done"), sem1("acc_done")
            rden_done, row_done = sem1("rden_done"), sem1("row_done")

            with nc.Block() as block:
                @block.sync
                def _(sp):
                    for i, (a, b) in list(enumerate(x1_pieces))[X1_FIRST_PIECES:]:
                        wait(sp, x1_init[i % 2], 16 * (i // 2))
                        sp.dma_start(x1[a:b, :], x[a:b, :]).then_inc(x1_init[i % 2], 16)
                    for i, (to, q, n) in enumerate(zero_pieces):
                        wait(sp, agg_zero[i % 2], 16 * (i // 2))
                        sp.dma_start(to, zeros[0:q, 0:n]).then_inc(agg_zero[i % 2], 16)

                @block.gpsimd
                def _(pool):
                    last_row = pool.to_reg(N - 1)

                    def gather(g, u):
                        wait_apart(pool, (gidx_ready, g + 1), (row_done, (g - RING + 1) * TPG))
                        for k in range(TPG):
                            for rows_to, col in ((xs, 0), (xd, 1)):
                                nc.gpsimd.indirect_dma_start(
                                    rows_to[:, u, k, :], None, x,
                                    bass.IndirectOffsetOnAxis(ap=slot_g[:, u, col, k:k + 1], axis=0),
                                    bounds_check=last_row, oob_is_err=False).then_inc(gathered[u], 16)

                    def scatter_rows(index, from_rows, u):
                        for k in range(TPG):
                            nc.gpsimd.indirect_dma_start(
                                x1, bass.IndirectOffsetOnAxis(ap=index[:, k:k + 1], axis=0),
                                from_rows[:, k, :], None, bounds_check=last_row,
                                oob_is_err=False).then_inc(scattered[u], 16)

                    def scatter(g, u):
                        if isinstance(g, int) and g < EARLY:
                            if g == EARLY - 1:
                                for i in range(2):
                                    pool.wait_ge(x1_init[i], 16 * len(x1_pieces[i::2]))
                                pool.wait_ge(row_done, EARLY * TPG)
                                for e in range(EARLY):
                                    scatter_rows(early_index[:, e, :], early_rows[:, e, :, :], e % RING)
                            return
                        wait_apart(pool, (row_done, (g + 1) * TPG))
                        scatter_rows(slot_s[:, u, :], rows[:, u, :, :], u)
                    pipeline(pool, (gather, 3), (scatter, -1), peel=EARLY + 1)
                    for u in range(RING):
                        pool.wait_ge(scattered[u], 16 * TPG * len(range(u, G, RING)))

                @block.scalar
                def _(act):
                    def center(g, u):
                        wait(act, mean_done, g + 1)
                        wait(act, u_done, (g - RING + 1) * TPG)
                        wait(act, dot_done, (g - 1) * TPG)
                        for k in range(TPG):
                            for j, (a, h) in enumerate(((xs, hs[:, u, k, 0:D]), (xd, hd[:, u % 2, k, :]))):
                                nc.scalar.activation(h, a[:, u, k, :], ACT.Relu,
                                                     bias=neg_mean[:, u % 2, j, k:k + 1]).then_inc(h_done, 1)

                    def squares(g, u, tiles):
                        wait(act, rs_in_done, g - 1)
                        for k in tiles:
                            for j, h in enumerate((hs[:, u, k, 0:D], hd[:, u % 2, k, :])):
                                wait(act, h_done, g * 2 * TPG + 2 * k + j + 1)
                                wait(act, sq_done, g * 2 * TPG + 2 * k + j - 1)
                                nc.scalar.activation(junk_a[:, j, :], h, ACT.Square,
                                                     accum_out=sq[:, u % 2, j, k:k + 1]).then_inc(sq_done, 1)

                    def early_squares(g, u):
                        squares(g, u, range(0, TPG // 2))

                    def late_squares(g, u):
                        squares(g, u, range(TPG // 2, TPG))

                    def weigh(g, u):
                        wait(act, ev_done, g + 1)
                        wait(act, acc_done, (g - 1) * TPG)
                        nc.scalar.activation(pw[:, u % 2, :, :], ev[:, :, :], ACT.Exp).then_inc(pw_done, 1)

                    def parts(g, u):
                        for k in range(TPG):
                            wait(act, u_done, g * TPG + k + 1)
                            wait(act, acc_done, g * TPG + k - 1)
                            nc.scalar.copy(part[:, k % 2, :], U_ps[k % 2][:, 0:AUG]).then_inc(part_done, 1)
                    pipeline(act, (weigh, 0), (late_squares, 1), (parts, 0), (center, 2), (early_squares, 2))

                @block.vector
                def _(dve):
                    nc.vector.memset(acc[:, TPG - 1, :], 0.0).then_inc(carry_set, 1)
                    nc.vector.memset(carry[:, 0:1], 0.0).then_inc(carry_kept, 1)

                    def gather_indices(g, u):
                        wait(dve, gathered[u], laps(g, u, 32 * TPG) - 32 * TPG)
                        gather_slots(g, u, gidx_ready)

                    def targets(g, u):
                        if isinstance(g, int) and g < EARLY:
                            nc.vector.tensor_copy(early_index[:, g, :], edge_i[:, g, 2, :])
                        else:
                            scatter_slots(g, u, None if isinstance(g, int) and g < EARLY + RING else scattered)

                    def segments(g, u):
                        segment_slots(g, u, seg_ready)

                    def statistics(g, u, k):
                        if k == 0:
                            wait(dve, gathered[u], laps(g, u, 32 * TPG))
                            wait(dve, mv_done, g)
                        for j, a in enumerate((xs, xd)):
                            n = nc.vector.bn_stats(st6[:, j, k, :], a[:, u, k, :])
                        if k == TPG - 1:
                            n.then_inc(st_done, 1)

                    def first_statistics(g, u):
                        if isinstance(g, int) and g < 2:
                            for k in range(TPG):
                                statistics(g, u, k)
                            moments(g, u)

                    def moments(g, u):
                        wait_apart(dve, (st_done, g + 1), (v_eps_done, 2 * g))
                        for j in range(2):
                            for k in range(TPG):
                                n = nc.vector.bn_aggr(mv[:, j, k, :], st6[:, j, k, :])
                        n.then_inc(mv_done, 1)
                        wait(dve, mv_done, g + 1)
                        wait(dve, h_done, (g - 1) * 2 * TPG)
                        nc.vector.tensor_scalar(neg_mean[:, u % 2, :, :], mv[:, :, :, 0], -1.0, None,
                                                ALU.mult).then_inc(mean_done, 1)
                        wait(dve, rs_in_done, g - 1)
                        nc.vector.tensor_scalar(var_eps[:, u % 2, :, :], mv[:, :, :, 1], LN_EPS, None,
                                                ALU.add).then_inc(v_eps_done, 1)
                        wait(dve, aug_done, g - RING + 1)
                        nc.vector.tensor_scalar(rs_in[:, u, 2, :], mv[:, 0, :, 1], LN_EPS, None,
                                                ALU.add).then_inc(v_eps_done, 1)

                    def product(g, u, k):
                        wait(dve, h_done, g * 2 * TPG + 2 * k + 2)
                        wait(dve, dot_done, g * TPG + k)
                        nc.vector.tensor_tensor_reduce(junk_v[:, :], hs[:, u, k, 0:D], hd[:, u % 2, k, :], 1.0, 0.0,
                                                       ALU.mult, ALU.add,
                                                       accum_out=dot[:, u % 2, k:k + 1]).then_inc(dot_done, 1)

                    def squared_norms(g, u):
                        wait(dve, sq_done, (g + 1) * 2 * TPG)
                        wait(dve, v_eps_done, 2 * g + 2)
                        nc.vector.scalar_tensor_tensor(rs_in[:, u, 0:2, :], var_eps[:, u % 2, :, :],
                                                       NORM_EPS * NORM_EPS, sq[:, u % 2, :, :], ALU.mult,
                                                       ALU.max).then_inc(rs_in_done, 1)

                    def root(g, u, i):
                        if i == 0:
                            wait(dve, rs_in_done, g + 1)
                            wait(dve, p_rstd_done, g - 1)
                        rsqrt_step(dve, i, rs[:, u % 2, :, :], rs_in[:, u, :, :], root_tmp[:, :, :], g * RSQRT_STEPS,
                                   rs_done)

                    def penalty(g, u, k):
                        wait(dve, drow_done, g + 1)
                        wait(dve, tmax_done, g * TPG)
                        nc.vector.tensor_scalar(pen[:, k, :], D_ps[u % 2][:, k * P:(k + 1) * P],
                                                slot_f[:, u, 0, k:k + 1], LOWEST, ALU.not_equal,
                                                ALU.mult).then_inc(pen_done, 1)

                    def half_scores(g, u):
                        wait(dve, rs_done, (g + 1) * RSQRT_STEPS)
                        wait(dve, dot_done, (g + 1) * TPG)
                        wait(dve, score_done, g)
                        nc.vector.scalar_tensor_tensor(half[:, :], dot[:, u % 2, :], params[:, 6:7],
                                                       rs[:, u % 2, 0, :], ALU.mult, ALU.mult).then_inc(half_done, 1)

                    def scores(g, u):
                        wait(dve, half_done, g + 1)
                        wait(dve, erow_done, g - 1)
                        nc.vector.tensor_tensor(score[:, u % 2, :], half[:, :], rs[:, u % 2, 1, :],
                                                ALU.mult).then_inc(score_done, 1)
                        nc.vector.tensor_tensor(hs[:, u, :, D], rs_in[:, u, 2, :], rs[:, u % 2, 2, :],
                                                ALU.mult).then_inc(aug_done, 1)

                    def first_scores(g, u):
                        if isinstance(g, int) and g == 0:
                            for k in range(TPG):
                                product(g, u, k)
                            squared_norms(g, u)
                            for i in range(RSQRT_STEPS):
                                root(g, u, i)
                            for k in range(TPG):
                                penalty(g, u, k)
                            half_scores(g, u)
                            scores(g, u)

                    def weights(g, u):
                        s, more = u % 2, not is_tail(g)
                        after = (g + 1, (u + 1) % RING)
                        wait_apart(dve, (erow_done, g + 1), (last_row_done, g), (max_done, g), (pen_done, (g + 1) * TPG))
                        for k in range(TPG):
                            nc.vector.tensor_tensor_reduce(pen[:, k, :], pen[:, k, :], E_ps[s][:, k * P:(k + 1) * P],
                                                           1.0, LOWEST, ALU.add, ALU.max,
                                                           accum_out=tile_max[:, k:k + 1]).then_inc(tmax_done, 1)
                        for k in range(TPG - 1):
                            if more:
                                product(*after, k)
                        wait(dve, last_row_done, g + 1)
                        wait(dve, carry_kept, g + 1)
                        nc.vector.tensor_tensor_scan(carry[:, 1:1 + TPG], slot_f[:, u, 3, :], M_ps[:, 0:TPG],
                                                     carry[:, 0:1], ALU.add, ALU.max).then_inc(carry_done, 1)
                        if more:
                            product(*after, TPG - 1)
                        wait(dve, carry_done, g + 1)
                        wait(dve, ev_done, g)
                        nc.vector.tensor_tensor(carried[:, :], carry[:, 0:TPG], slot_f[:, u, 1, :],
                                                ALU.add).then_inc(carried_done, 1)
                        wait(dve, carried_done, g + 1)
                        wait(dve, tmax_done, (g + 1) * TPG)
                        nc.vector.tensor_tensor(smax[:, :], tile_max[:, :], carried[:, :], ALU.max).then_inc(max_done, 1)
                        nc.vector.tensor_copy(carry[:, 0:1], carry[:, TPG:TPG + 1]).then_inc(carry_kept, 1)
                        wait(dve, max_done, g + 1)
                        wait(dve, pw_done, g)
                        nc.vector.tensor_tensor(ev[:, 0, :], score[:, s, :], smax[:, :], ALU.subtract)
                        nc.vector.tensor_tensor(ev[:, 1, :], carried[:, :], smax[:, :],
                                                ALU.subtract).then_inc(ev_done, 1)
                        if not isinstance(g, int) or g + 2 < G:
                            statistics(g + 2, (u + 2) % RING, 0)
                        wait(dve, pw_done, g + 1)
                        wait(dve, wsel_done, g * TPG)
                        nc.vector.tensor_tensor(p_rstd[:, :], pw[:, s, 0, :], rs[:, s, 2, :],
                                                ALU.mult).then_inc(p_rstd_done, 1)
                        wait(dve, p_rstd_done, g + 1)
                        wait(dve, u_done, g * TPG)
                        for k in range(TPG):
                            nc.vector.tensor_scalar(wsel[:, k, :], D_ps[s][:, k * P:(k + 1) * P],
                                                    slot_f[:, u, 0, k:k + 1], p_rstd[:, k:k + 1], ALU.is_equal,
                                                    ALU.mult).then_inc(wsel_done, 1)
                        if more:
                            squared_norms(*after)

                    def sums(g, u):
                        more, more2 = not is_tail(g), not isinstance(g, int) or g + 2 < G
                        after, after2 = (g + 1, (u + 1) % RING), (g + 2, (u + 2) % RING)
                        wait(dve, row_done, g * TPG)
                        if more:
                            root(*after, 0)
                        for k in range(TPG):
                            wait(dve, cu_done, g * TPG + k + 1)
                            wait(dve, part_done, g * TPG + k + 1)
                            nc.vector.scalar_tensor_tensor(acc[:, k, :], C_ps[:, 0:AUG], pw[:, u % 2, 1, k:k + 1],
                                                           part[:, k % 2, :], ALU.mult, ALU.add).then_inc(acc_done, 1)
                            if more and k < TPG - 1:
                                root(*after, 3 * k + 1)
                                penalty(*after, k)
                                root(*after, 3 * k + 2)
                                if more2:
                                    statistics(*after2, k + 1)
                                root(*after, 3 * k + 3)
                            elif more:
                                half_scores(*after)
                                penalty(*after, k)
                                scores(*after)
                                if more2:
                                    moments(*after2)
                        wait(dve, acc_done, (g + 1) * TPG)
                        nc.vector.reciprocal(rden[:, :], acc[:, :, D]).then_inc(rden_done, 1)
                        early = isinstance(g, int) and g < EARLY
                        if not isinstance(g, int) or g >= EARLY + RING:
                            wait(dve, scattered[u], laps(g, u, 16 * TPG) - 16 * TPG)
                        wait(dve, rden_done, g + 1)
                        for k in range(TPG):
                            row = early_rows[:, g, k, :] if early else rows[:, u, k, :]
                            nc.vector.scalar_tensor_tensor(row, acc[:, k, 0:D], rden[:, k:k + 1],
                                                           xd[:, u, k, :], ALU.mult, ALU.add).then_inc(row_done, 1)
                    pipeline(dve, (gather_indices, 3), (segments, 2), (targets, 1), (first_statistics, 2),
                             (first_scores, 1), (weights, 0), (sums, 0), peel=EARLY + RING)

                @block.tensor
                def _(pe):
                    def dst_rows(g, u):
                        wait(pe, seg_ready, g + 1)
                        wait(pe, wsel_done, (g - 1) * TPG)
                        for k in range(TPG):
                            n = nc.tensor.matmul(D_ps[u % 2][:, k * P:(k + 1) * P],
                                                 slot_f[:, u, 0, k:k + 1].broadcast_to([P, P]), ident[:, :],
                                                 start=True, stop=True)
                        n.then_inc(drow_done, 1)

                    def score_rows(g, u):
                        s = u % 2
                        wait(pe, score_done, g + 1)
                        wait(pe, tmax_done, (g - 1) * TPG)
                        for k in range(TPG):
                            n = nc.tensor.matmul(E_ps[s][:, k * P:(k + 1) * P],
                                                 score[:, s, k:k + 1].broadcast_to([P, P]), ident[:, :],
                                                 start=True, stop=True)
                        n.then_inc(erow_done, 1)

                    def last_maxima(g, u):
                        wait(pe, tmax_done, (g + 1) * TPG)
                        wait(pe, carry_done, g)
                        nc.tensor.matmul(M_ps[:, 0:TPG], pick_last[:, :], tile_max[:, :], start=True,
                                         stop=True).then_inc(last_row_done, 1)

                    def segment_sums(g, u):
                        wait(pe, aug_done, g + 1)
                        if isinstance(g, int) and g == 0:
                            pe.wait_ge(carry_set, 1)
                        for k in range(TPG):
                            wait(pe, wsel_done, g * TPG + k + 1)
                            wait(pe, part_done, g * TPG + k - 1)
                            nc.tensor.matmul(U_ps[k % 2][:, 0:AUG], wsel[:, k, :], hs[:, u, k, :], start=True,
                                             stop=True).then_inc(u_done, 1)
                            wait(pe, acc_done, g * TPG + k)
                            nc.tensor.matmul(C_ps[:, 0:AUG], pick_last[:, :], acc[:, (k - 1) % TPG, :], start=True,
                                             stop=True).then_inc(cu_done, 1)
                    pipeline(pe, (last_maxima, 0), (dst_rows, 1), (segment_sums, 0), (score_rows, 1))

        y_kept = sb("y_kept", [P, -(-G // RING) * KEPT * GW])
        y_slot = sb("y_slot", [P, RING - KEPT, GW])

        def y_tile(g, u):
            if u < KEPT:
                return y_kept[:, bass.ds((g - u) * (GW // RING * KEPT) + u * GW, GW)]
            return y_slot[:, u - KEPT, :]

        def spilled(g):
            return y_spilled[:, bass.ds(g * GW, GW)]

        def mlp_front(tag, gather_rows, side, side_sorted, w_sb, bias_col):
            with ExitStack() as c1:
                def sb1(name, shape, dt=fp32):
                    return c1.enter_context(nc.sbuf_tensor(tag + name, shape, dt))

                pass_sems = []

                def sem1(name):
                    pass_sems.append(nc.alloc_semaphore(name=tag + name))
                    return pass_sems[-1]
                xs = sb1("xs", [P, RING, TPG, D])
                sd = sb1("sd", [P, RING, TPG, D])
                hs = sb1("hs", [P, 2, TPG, D])
                hT = sb1("hT", [P, 2, GW])
                sT = sb1("sT", [P, 2, GW])
                st6 = sb1("st6", [P, TPG, 6])
                mv = sb1("mv", [P, 2, TPG, 2])
                var_eps = sb1("var_eps", [P, 2, TPG])
                rstd = sb1("rstd", [P, 2, TPG])
                shift = sb1("shift", [P, 2, TPG])
                root_tmp = sb1("root_tmp", [P, TPG])
                idx_ready = sem1("idx_ready")
                rows_in = [sem1(f"rows_in{u}") for u in range(RING)]
                side_in = [sem1(f"side_in{u}") for u in range(RING)]
                y_out = {u: sem1(f"y_out{u}") for u in range(KEPT, RING)}
                st_done, mv_done, v_eps_done, rstd_done, shift_done = (
                    sem1(n) for n in ("st_done", "mv_done", "v_eps_done", "rstd_done", "shift_done"))
                h_done, hT_ps_done, sT_ps_done = sem1("h_done"), sem1("hT_ps_done"), sem1("sT_ps_done")
                hT_done, sT_done, y_ps_done, y_done, bn_done = (
                    sem1(n) for n in ("hT_done", "sT_done", "y_ps_done", "y_done", "bn_done"))
                row_dmas = TPG if gather_rows else 1
                root_steps = RSQRT_STEPS if gather_rows else 1

                with nc.Block() as block:
                    @block.sync
                    def _(sp):
                        if gather_rows:
                            unsorted_flag = sp.value_load(unsorted[0:1, 0:1], min_val=0, max_val=1)

                        def load_side(g, u):
                            wait_apart(sp, (sT_ps_done, g - RING + 1))
                            if gather_rows:
                                with sp.If(unsorted_flag > 0):
                                    for a, b in row_moves(side_sorted, sd[:, u, :, :], g, True):
                                        sp.dma_start(a, b).then_inc(side_in[u], 16)
                                with sp.Else():
                                    for a, b in row_moves(side, sd[:, u, :, :], g, True):
                                        sp.dma_start(a, b).then_inc(side_in[u], 16)
                                sp.end_ifs()
                                return
                            for a, b in row_moves(side, sd[:, u, :, :], g, True):
                                sp.dma_start(a, b).then_inc(side_in[u], 16)

                        def load_rows(g, u):
                            wait_apart(sp, (h_done, g - RING + 1))
                            for a, b in row_moves(x1, xs[:, u, :, :], g, True):
                                sp.dma_start(a, b).then_inc(rows_in[u], 16)

                        def store_y(g, u):
                            if u >= KEPT:
                                wait_apart(sp, (y_done, g + 1))
                                sp.dma_start(spilled(g), y_tile(g, u)).then_inc(y_out[u], 16)
                        if gather_rows:
                            pipeline(sp, (load_side, 2), (store_y, -2))
                        else:
                            pipeline(sp, (load_rows, 4), (load_side, 2), (store_y, -2))
                        for u in range(KEPT, RING):
                            sp.wait_ge(y_out[u], 16 * len(range(u, G, RING)))

                    @block.gpsimd
                    def _(pool):
                        last_row = pool.to_reg(N - 1) if gather_rows else None

                        def gather(g, u):
                            wait_apart(pool, (idx_ready, g + 1), (h_done, g - RING + 1))
                            for k in range(TPG):
                                nc.gpsimd.indirect_dma_start(
                                    xs[:, u, k, :], None, x1,
                                    bass.IndirectOffsetOnAxis(ap=slot_g[:, u, 0, k:k + 1], axis=0),
                                    bounds_check=last_row, oob_is_err=False).then_inc(rows_in[u], 16)

                        def rsqrt(g, u):
                            wait(pool, v_eps_done, g + 1)
                            wait(pool, h_done, g - 1)
                            wait(pool, shift_done, g - 1)
                            nc.gpsimd.tensor_tensor(rstd[:, u % 2, :], var_eps[:, u % 2, :],
                                                    minus_half[:, 0:TPG], ALU.pow).then_inc(rstd_done, 1)
                        if gather_rows:
                            pipeline(pool, (gather, 4))
                        else:
                            pipeline(pool, (rsqrt, 3))

                    @block.scalar
                    def _(act):
                        def normalise(g, u):
                            wait(act, shift_done, g + 1)
                            wait(act, hT_ps_done, g - 1)
                            for k in range(TPG):
                                n = nc.scalar.activation(hs[:, u % 2, k, :], xs[:, u, k, :], ACT.Relu,
                                                         bias=shift[:, u % 2, k:k + 1],
                                                         scale=rstd[:, u % 2, k:k + 1])
                            n.then_inc(h_done, 1)

                        def copy_side(g, u):
                            wait(act, sT_ps_done, g + 1)
                            wait(act, y_ps_done, g - 1)
                            nc.scalar.copy(sT[:, u % 2, :], ps[2 + u % 2][:, :]).then_inc(sT_done, 1)

                        def add_bias(g, u):
                            wait(act, y_ps_done, g + 1)
                            if u >= KEPT:
                                wait(act, y_out[u], laps(g, u, 16) - 16)
                                wait(act, bn_done, g - RING + 1)
                            nc.scalar.activation(y_tile(g, u), ps[4 + u % 2][:, :], ACT.Identity,
                                                 bias=params[:, bias_col:bias_col + 1], scale=1.0).then_inc(y_done, 1)
                        pipeline(act, (add_bias, -2), (normalise, 1), (copy_side, 0))

                    @block.vector
                    def _(dve):
                        def slots(g, u):
                            wait(dve, rows_in[u], laps(g, u, 16 * TPG) - 16 * TPG)
                            gather_slots(g, u, idx_ready)

                        def root(i):
                            def part(g, u):
                                if i == 0:
                                    wait(dve, v_eps_done, g + 1)
                                    wait(dve, h_done, g - 1)
                                    wait(dve, shift_done, g - 1)
                                rsqrt_step(dve, i, rstd[:, u % 2, :], var_eps[:, u % 2, :], root_tmp[:, :],
                                           g * RSQRT_STEPS, rstd_done)
                            return part

                        def statistics(k):
                            def part(g, u):
                                if k == 0:
                                    wait(dve, rows_in[u], laps(g, u, 16 * row_dmas)
                                         + (16 if is_tail(g) and not gather_rows else 0))
                                    wait(dve, mv_done, g)
                                n = nc.vector.bn_stats(st6[:, k, :], xs[:, u, k, :])
                                if k == TPG - 1:
                                    n.then_inc(st_done, 1)
                            return part

                        def moments(g, u):
                            wait_apart(dve, (st_done, g + 1), (shift_done, g - 1))
                            for k in range(TPG):
                                n = nc.vector.bn_aggr(mv[:, u % 2, k, :], st6[:, k, :])
                            n.then_inc(mv_done, 1)

                        def variances(g, u):
                            wait(dve, mv_done, g + 1)
                            wait(dve, rstd_done, (g - 1) * root_steps)
                            nc.vector.tensor_scalar(var_eps[:, u % 2, :], mv[:, u % 2, :, 1], LN_EPS, None,
                                                    ALU.add).then_inc(v_eps_done, 1)

                        def shifts(g, u):
                            wait(dve, rstd_done, (g + 1) * root_steps)
                            wait(dve, h_done, g - 1)
                            nc.vector.scalar_tensor_tensor(shift[:, u % 2, :], mv[:, u % 2, :, 0], -1.0,
                                                           rstd[:, u % 2, :], ALU.mult,
                                                           ALU.mult).then_inc(shift_done, 1)

                        def copy_h(g, u):
                            wait(dve, hT_ps_done, g + 1)
                            wait(dve, y_ps_done, g - 1)
                            nc.vector.tensor_copy(hT[:, u % 2, :], ps[u % 2][:, :]).then_inc(hT_done, 1)

                        def count_y(g, u):
                            wait(dve, y_done, g + 1)
                            n = TAIL if is_tail(g) else GW
                            nc.vector.bn_stats(bn_sum[:, bass.ds(g, 1), :].rearrange("p o c -> p (o c)"),
                                               y_tile(g, u)[:, 0:n]).then_inc(bn_done, 1)
                        if gather_rows:
                            pipeline(dve, (root(0), 2), (shifts, 1), (statistics(0), 3), (root(1), 2),
                                     (statistics(1), 3), (root(2), 2), (statistics(2), 3), (root(3), 2),
                                     (statistics(3), 3), (root(4), 2), (slots, 5), (root(5), 2), (copy_h, 0),
                                     (root(6), 2), (moments, 3), (root(7), 2), (variances, 3), (root(8), 2),
                                     (count_y, -2), (root(9), 2))
                        else:
                            pipeline(dve, (statistics(0), 3), (statistics(1), 3), (statistics(2), 3), (statistics(3), 3),
                                     (shifts, 2), (copy_h, 0), (moments, 3), (variances, 3), (count_y, -2))

                    @block.tensor
                    def _(pe):
                        def turn_side(g, u):
                            wait(pe, side_in[u], laps(g, u, 16) + (16 if is_tail(g) else 0))
                            wait(pe, sT_done, g - 1)
                            for k in range(TPG):
                                n = nc.tensor.transpose(ps[2 + u % 2][:, k * P:(k + 1) * P], sd[:, u, k, :],
                                                        ident[:, :])
                            n.then_inc(sT_ps_done, 1)

                        def turn_h(g, u):
                            wait(pe, h_done, g + 1)
                            wait(pe, hT_done, g - 1)
                            for k in range(TPG):
                                n = nc.tensor.transpose(ps[u % 2][:, k * P:(k + 1) * P], hs[:, u % 2, k, :],
                                                        ident[:, :])
                            n.then_inc(hT_ps_done, 1)

                        def product(g, u):
                            wait(pe, hT_done, g + 1)
                            wait(pe, sT_done, g + 1)
                            wait(pe, y_done, g - 1)
                            nc.tensor.matmul(ps[4 + u % 2][:, :], w_sb[:, 0, :], hT[:, u % 2, :], start=True, stop=False)
                            nc.tensor.matmul(ps[4 + u % 2][:, :], w_sb[:, 1, :], sT[:, u % 2, :], start=False,
                                             stop=True).then_inc(y_ps_done, 1)
                        pipeline(pe, (turn_side, 0), (turn_h, 0), (product, -1))
                nc.clear_and_free_semaphores(pass_sems)
                nc.all_engine_barrier()

        def bn_coefficients(pool, dve, var_ready, inv_ready, step, gamma_col, beta_col):
            if dve is None:
                pool.wait_ge(var_ready, 1)
                nc.gpsimd.tensor_scalar(bn_rstd[:, :], bn_mv[:, 1:2], BN_EPS, None, ALU.add).then_inc(inv_ready, 1)
                pool.wait_ge(inv_ready, 1)
                nc.gpsimd.tensor_tensor(bn_rstd[:, :], bn_rstd[:, :], minus_half[:, 0:1], ALU.pow).then_inc(inv_ready, 1)
                return
            nc.vector.bn_aggr(bn_mv[:, :], bn_sum[:, :, :].rearrange("p g c -> p (g c)")).then_inc(var_ready, 1)
            dve.wait_ge(var_ready, 1)
            dve.wait_ge(inv_ready, 2)
            nc.vector.tensor_tensor(bn_s[:, :], bn_rstd[:, :], params[:, gamma_col:gamma_col + 1], ALU.mult).then_inc(step, 1)
            dve.wait_ge(step, 1)
            nc.vector.tensor_tensor(bn_tmp[:, :], bn_mv[:, 0:1], bn_s[:, :], ALU.mult).then_inc(step, 1)
            dve.wait_ge(step, 2)
            nc.vector.tensor_tensor(bn_t[:, :], params[:, beta_col:beta_col + 1], bn_tmp[:, :],
                                    ALU.subtract).then_inc(step, 1)

        mlp_front("p2_", True, edge_attr, ea_sorted, w1_sb, 0)

        with ExitStack() as c1:
            def sb1(name, shape, dt=fp32):
                return c1.enter_context(nc.sbuf_tensor("p3_" + name, shape, dt))

            def sem1(name):
                return c1.enter_context(nc.semaphore("p3_" + name))
            ex = sb1("ex", [P, 2, GW])
            rl = sb1("rl", [P, 2, GW])
            el = sb1("el", [P, 2, GW])
            h1 = sb1("h1", [P, 2, TPG, AUG])
            sel = sb1("sel", [P, 2, TPG, D])
            part = sb1("part", [P, 2, AUG])
            acc = sb1("acc", [P, 2, TPG, AUG])
            cnt = sb1("cnt", [P, TPG])
            rden = sb1("rden", [P, 2, TPG])
            rows = sb1("rows", [P, RING, TPG, D])
            D_ps, T_ps, U_ps, C_ps = [ps[0], ps[1]], [ps[2], ps[3]], [ps[4], ps[5]], ps[6]
            init_set, bn_var, bn_inv, bn_step, idx_ready = (
                sem1(n) for n in ("init_set", "bn_var", "bn_inv", "bn_step", "idx_ready"))
            y_in = {u: sem1(f"y_in{u}") for u in range(KEPT, RING)}
            scattered = [sem1(f"scattered{u}") for u in range(RING)]
            ex_done, rl_done, el_done, elT_done, h1_done = (
                sem1(n) for n in ("ex_done", "rl_done", "el_done", "elT_done", "h1_done"))
            drow_done, sel_done, u_done, part_done, cu_done = (
                sem1(n) for n in ("drow_done", "sel_done", "u_done", "part_done", "cu_done"))
            acc_done, cnt_done, rden_done, row_done = (
                sem1(n) for n in ("acc_done", "cnt_done", "rden_done", "row_done"))

            with nc.Block() as block:
                @block.sync
                def _(sp):
                    def load_y(g, u):
                        if u >= KEPT:
                            wait_apart(sp, (rl_done, g - RING + 1))
                            sp.dma_start(y_tile(g, u), spilled(g)).then_inc(y_in[u], 16)
                    pipeline(sp, (load_y, 4))

                @block.gpsimd
                def _(pool):
                    last_row = pool.to_reg(N - 1)
                    bn_coefficients(pool, None, bn_var, bn_inv, bn_step, 1, 2)

                    for i in range(2):
                        pool.wait_ge(agg_zero[i], 16 * len(zero_pieces[i::2]))

                    def scatter(g, u):
                        for k in range(TPG):
                            if k % 2 == 0:
                                wait_apart(pool, (row_done, g * TPG + k + 2))
                            nc.gpsimd.indirect_dma_start(
                                agg, bass.IndirectOffsetOnAxis(ap=slot_s[:, u, k:k + 1], axis=0),
                                rows[:, u, k, :], None, bounds_check=last_row,
                                oob_is_err=False).then_inc(scattered[u], 16)
                    pipeline(pool, (scatter, 0))
                    for u in range(RING):
                        pool.wait_ge(scattered[u], 16 * TPG * len(range(u, G, RING)))

                @block.scalar
                def _(act):
                    act.wait_ge(bn_step, 3)

                    def exponential(g, u):
                        if u >= KEPT:
                            wait(act, y_in[u], laps(g, u, 16))
                        wait(act, el_done, g - 1)
                        nc.scalar.activation(ex[:, u % 2, :], y_tile(g, u), ACT.Exp, bias=bn_t[:, :],
                                             scale=bn_s[:, :]).then_inc(ex_done, 1)

                    def linear(g, u):
                        nc.scalar.activation(rl[:, u % 2, :], y_tile(g, u), ACT.Relu, bias=bn_t[:, :],
                                             scale=bn_s[:, :]).then_inc(rl_done, 1)

                    def edge_major(g, u):
                        wait(act, elT_done, g + 1)
                        wait(act, u_done, (g - 1) * TPG)
                        if isinstance(g, int) and g < 2:
                            wait(act, init_set, 2)
                        nc.scalar.activation(h1[:, u % 2, :, 0:D],
                                             T_ps[u % 2][:, :].rearrange("p (k f) -> p k f", k=TPG),
                                             ACT.Copy, bias=-1.0).then_inc(h1_done, 1)

                    def part_of(k):
                        def copy(g, u):
                            wait(act, u_done, g * TPG + k + 1)
                            wait(act, acc_done, g * TPG + k - 1)
                            nc.scalar.copy(part[:, k % 2, :], U_ps[k % 2][:, 0:AUG]).then_inc(part_done, 1)
                        return copy
                    pipeline(act, (part_of(0), 0), (exponential, 3), (part_of(1), 0), (edge_major, 1), (part_of(2), 0),
                             (linear, 3), (part_of(3), 0))

                @block.vector
                def _(dve):
                    bn_coefficients(None, dve, bn_var, bn_inv, bn_step, 1, 2)
                    nc.vector.memset(h1[:, :, :, D:AUG], 1.0).then_inc(init_set, 1)
                    nc.vector.memset(acc[:, 1, TPG - 1, :], 0.0).then_inc(init_set, 1)

                    def slots(g, u):
                        segment_slots(g, u, idx_ready)

                    def targets(g, u):
                        scatter_slots(g, u, scattered)

                    def join(g, u, k):
                        if k == 0:
                            wait(dve, ex_done, g + 1)
                            wait(dve, rl_done, g + 1)
                            wait(dve, elT_done, g - 1)
                        c = slice(k * P, (k + 1) * P)
                        n = nc.vector.scalar_tensor_tensor(el[:, u % 2, c], ex[:, u % 2, c], 1.0, rl[:, u % 2, c],
                                                           ALU.min, ALU.add)
                        if k == TPG - 1:
                            n.then_inc(el_done, 1)

                    def first_joins(g, u):
                        if isinstance(g, int) and g < 2:
                            for k in range(TPG):
                                join(g, u, k)

                    def selector(g, u, k):
                        wait(dve, drow_done, g + 1)
                        wait(dve, idx_ready, g + 1)
                        wait(dve, u_done, (g - 1) * TPG)
                        nc.vector.tensor_scalar(sel[:, u % 2, k, :], D_ps[u % 2][:, k * P:(k + 1) * P],
                                                slot_f[:, u, 0, k:k + 1], None,
                                                ALU.is_equal).then_inc(sel_done, 1)

                    def first_selectors(g, u):
                        if isinstance(g, int) and g == 0:
                            for k in range(TPG):
                                selector(g, u, k)

                    def counts(g, u):
                        wait(dve, acc_done, (g + 1) * TPG)
                        wait(dve, rden_done, g)
                        nc.vector.tensor_scalar(cnt[:, :], acc[:, u % 2, :, D], 1.0, None, ALU.max).then_inc(cnt_done, 1)

                    def inverse_counts(g, u):
                        wait(dve, cnt_done, g + 1)
                        nc.vector.reciprocal(rden[:, u % 2, :], cnt[:, :]).then_inc(rden_done, 1)

                    def row(g, u, k):
                        if k == 0:
                            wait(dve, rden_done, g + 1)
                            wait(dve, scattered[u], laps(g, u, 16 * TPG) - 16 * TPG)
                        nc.vector.tensor_scalar(rows[:, u, k, :], acc[:, u % 2, k, 0:D], rden[:, u % 2, k:k + 1], None,
                                                ALU.mult).then_inc(row_done, 1)

                    def means(g, u):
                        wait(dve, row_done, (g - 1) * TPG)
                        for k in range(TPG):
                            wait(dve, cu_done, g * TPG + k + 1)
                            wait(dve, part_done, g * TPG + k + 1)
                            nc.vector.scalar_tensor_tensor(acc[:, u % 2, k, :], C_ps[:, 0:AUG],
                                                           slot_f[:, u, 2, k:k + 1], part[:, k % 2, :], ALU.mult,
                                                           ALU.add).then_inc(acc_done, 1)
                            if not is_tail(g):
                                selector(g + 1, (u + 1) % RING, k)
                            if k == TPG - 1:
                                counts(g, u)
                            if not isinstance(g, int) or g + 2 < G:
                                join(g + 2, (u + 2) % RING, k)
                            if k == TPG - 1:
                                inverse_counts(g, u)
                            if not isinstance(g, int) or g > 0:
                                row(g - 1, (u - 1) % RING, k)

                    def last_rows(g, u):
                        if is_tail(g):
                            for k in range(TPG):
                                row(g, u, k)
                    pipeline(dve, (slots, 2), (targets, 0), (first_joins, 2), (first_selectors, 1), (means, 0),
                             (last_rows, 0))

                @block.tensor
                def _(pe):
                    pe.wait_ge(init_set, 2)

                    def dst_rows(tiles):
                        def rows(g, u):
                            if tiles[0] == 0:
                                wait(pe, idx_ready, g + 1)
                                wait(pe, sel_done, (g - 1) * TPG)
                            for k in tiles:
                                n = nc.tensor.matmul(D_ps[u % 2][:, k * P:(k + 1) * P],
                                                     slot_f[:, u, 0, k:k + 1].broadcast_to([P, P]), ident[:, :],
                                                     start=True, stop=True)
                            if tiles[-1] == TPG - 1:
                                n.then_inc(drow_done, 1)
                        return rows

                    def turn_el(g, u):
                        wait(pe, el_done, g + 1)
                        wait(pe, h1_done, g - 1)
                        for k in range(TPG):
                            n = nc.tensor.transpose(T_ps[u % 2][:, k * P:(k + 1) * P],
                                                    el[:, u % 2, k * P:(k + 1) * P], ident[:, :])
                        n.then_inc(elT_done, 1)

                    def segment_sum(k):
                        def part(g, u):
                            if k == 0:
                                wait(pe, h1_done, g + 1)
                            wait(pe, sel_done, g * TPG + k + 1)
                            wait(pe, part_done, g * TPG + k - 1)
                            nc.tensor.matmul(U_ps[k % 2][:, 0:AUG], sel[:, u % 2, k, :], h1[:, u % 2, k, :], start=True,
                                             stop=True).then_inc(u_done, 1)
                        return part

                    def carried_sum(k):
                        def part(g, u):
                            wait(pe, acc_done, g * TPG + k)
                            nc.tensor.matmul(C_ps[:, 0:AUG], pick_last[:, :],
                                             acc[:, (u - (k == 0)) % 2, (k - 1) % TPG, :], start=True,
                                             stop=True).then_inc(cu_done, 1)
                        return part
                    pipeline(pe, (carried_sum(0), 0), (segment_sum(1), 0), (turn_el, 1), (carried_sum(1), 0),
                             (segment_sum(2), 0), (dst_rows([0, 1]), 2), (carried_sum(2), 0), (segment_sum(3), 0),
                             (dst_rows([2, 3]), 2), (carried_sum(3), 0), (segment_sum(0), 1))

        mlp_front("p4_", False, agg, None, w2_sb, 3)

        with ExitStack() as c1:
            def sb1(name, shape, dt=fp32):
                return c1.enter_context(nc.sbuf_tensor("p5_" + name, shape, dt))

            def sem1(name):
                return c1.enter_context(nc.semaphore("p5_" + name))
            xr = sb1("xr", [P, RING, TPG, D])
            ex = sb1("ex", [P, 2, GW])
            rl = sb1("rl", [P, 2, GW])
            el = sb1("el", [P, 2, GW])
            res = sb1("res", [P, RING, TPG, D])
            bn_var, bn_inv, bn_step = sem1("bn_var"), sem1("bn_inv"), sem1("bn_step")
            y_in = {u: sem1(f"y_in{u}") for u in range(KEPT, RING)}
            x_in = [sem1(f"x_in{u}") for u in range(RING)]
            stored = [sem1(f"stored{u}") for u in range(RING)]
            ex_done, rl_done, el_done, elT_done, res_done = (
                sem1(n) for n in ("ex_done", "rl_done", "el_done", "elT_done", "res_done"))

            with nc.Block() as block:
                @block.sync
                def _(sp):
                    def load_y(g, u):
                        if u >= KEPT:
                            wait_apart(sp, (rl_done, g - RING + 1))
                            sp.dma_start(y_tile(g, u), spilled(g)).then_inc(y_in[u], 16)

                    def load_x(g, u):
                        wait_apart(sp, (res_done, g - RING + 1))
                        for a, b in row_moves(x1, xr[:, u, :, :], g, True):
                            sp.dma_start(a, b).then_inc(x_in[u], 16)

                    def store(g, u):
                        wait_apart(sp, (res_done, g + 1))
                        for a, b in row_moves(out, res[:, u, :, :], g, False):
                            sp.dma_start(a, b).then_inc(stored[u], 16)
                    pipeline(sp, (load_y, 4), (load_x, 2), (store, -1))
                    for u in range(RING):
                        sp.wait_ge(stored[u], 16 * (len(range(u, G, RING)) + (1 if u == (G - 1) % RING else 0)))

                @block.gpsimd
                def _(pool):
                    bn_coefficients(pool, None, bn_var, bn_inv, bn_step, 4, 5)

                @block.scalar
                def _(act):
                    act.wait_ge(bn_step, 3)

                    def branches(g, u):
                        if u >= KEPT:
                            wait(act, y_in[u], laps(g, u, 16))
                        wait(act, el_done, g - 1)
                        nc.scalar.activation(ex[:, u % 2, :], y_tile(g, u), ACT.Exp, bias=bn_t[:, :],
                                             scale=bn_s[:, :]).then_inc(ex_done, 1)
                        nc.scalar.activation(rl[:, u % 2, :], y_tile(g, u), ACT.Relu, bias=bn_t[:, :],
                                             scale=bn_s[:, :]).then_inc(rl_done, 1)
                    pipeline(act, (branches, 1))

                @block.vector
                def _(dve):
                    bn_coefficients(None, dve, bn_var, bn_inv, bn_step, 4, 5)

                    def join(g, u):
                        wait(dve, ex_done, g + 1)
                        wait(dve, rl_done, g + 1)
                        wait(dve, elT_done, g - 1)
                        nc.vector.scalar_tensor_tensor(el[:, u % 2, :], ex[:, u % 2, :], 1.0, rl[:, u % 2, :], ALU.min,
                                                       ALU.add).then_inc(el_done, 1)

                    def residual(g, u):
                        wait(dve, elT_done, g + 1)
                        wait(dve, x_in[u], laps(g, u, 16) + (16 if is_tail(g) else 0))
                        wait(dve, stored[u], laps(g, u, 16) - 16)
                        nc.vector.scalar_tensor_tensor(res[:, u, :, :].rearrange("p k f -> p (k f)"), ps[u % 2][:, :],
                                                       -1.0, xr[:, u, :, :].rearrange("p k f -> p (k f)"), ALU.add,
                                                       ALU.add).then_inc(res_done, 1)
                    pipeline(dve, (join, 1), (residual, 0))

                @block.tensor
                def _(pe):
                    def turn_el(g, u):
                        wait(pe, el_done, g + 1)
                        wait(pe, res_done, g - 1)
                        for k in range(TPG):
                            n = nc.tensor.transpose(ps[u % 2][:, k * P:(k + 1) * P], el[:, u % 2, k * P:(k + 1) * P],
                                                    ident[:, :])
                        n.then_inc(elT_done, 1)
                    pipeline(pe, (turn_el, 1))


_INS = ["x", "src", "dst", "edge_attr_128", "L0_gnn_beta", "L1_gnn_W1", "L1_gnn_b1", "L1_gnn_g1", "L1_gnn_be1",
        "L1_gnn_W2", "L1_gnn_b2", "L1_gnn_g2", "L1_gnn_be2"]


def kernel(**inputs):
    import numpy as np
    import concourse.bacc as bacc
    from concourse.bass_utils import run_bass_kernel_spmd

    nc = bacc.Bacc("TRN2", target_bir_lowering=False, num_devices=1)
    arrays, args = {}, []
    for name in _INS:
        a = np.ascontiguousarray(inputs[name])
        arrays[f"in_{name}"] = a
        args.append(nc.dram_tensor(f"in_{name}", a.shape, mybir.dt.from_np(a.dtype), kind="ExternalInput").ap())
    shape = inputs["x"].shape
    args.append(nc.dram_tensor("out_x", shape, mybir.dt.float32, kind="ExternalOutput").ap())
    build_gnn(nc, *args)
    r = run_bass_kernel_spmd(nc, [arrays], core_ids=[0])
    return r.results[0]["out_x"]
```
